# Optimizing a Trainium2 kernel written in Bass

```python
import numpy as np
import jax
import jax.numpy as jnp

def _softmax(x, axis=-1):
    return jax.nn.softmax(x, axis=axis)

def _gelu(x):
    return jax.nn.gelu(x, approximate=True)

def _silu(x):
    return jax.nn.silu(x)

def _sigmoid(x):
    return jax.nn.sigmoid(x)

def _layernorm(x, axis=-1, eps=1e-05):
    m = jnp.mean(x, axis=axis, keepdims=True)
    v = jnp.var(x, axis=axis, keepdims=True)
    return (x - m) / jnp.sqrt(v + eps)

def _scatter_add(tgt, idx, src, axis=0):
    return tgt.at[idx].add(src)

def _segment_sum(src, seg, n):
    return jax.ops.segment_sum(src, seg, n)
kernel_name = 'mk_adaln_ffn_d1_seqx_r4_936328'

def setup_inputs(seed: int=0):
    np.random.seed(seed)
    _w = jnp.asarray

    def _rec_inputs():
        import jax
        import jax.numpy as jnp
        _rk = jax.random.key(seed)
        x = -1.394e-06 + 0.9999 * jax.random.normal(jax.random.fold_in(_rk, 1), (16, 256, 512), jnp.float32)
        _lenS = 256 - jax.random.randint(jax.random.fold_in(_rk, 7), (16,), 0, max(1, 256 // 4) + 1, jnp.int32)
        _lenS2 = 256 - jax.random.randint(jax.random.fold_in(_rk, 8), (16,), 0, max(1, 256 // 4) + 1, jnp.int32)
        cond_2048 = -0.00499425 + 1.0058 * jax.random.normal(jax.random.fold_in(_rk, 11), (16, 512), jnp.float32)
        return (x, cond_2048)
    x, cond_2048 = _rec_inputs()

    def _L0_cond_setup():
        import jax, jax.numpy as jnp
        import numpy as np
        B, T, D = (16, 128, 512)
        key = jax.random.key(seed)
        k0, k1, k2, k3 = jax.random.split(key, 4)
        scale = 1.0 / np.sqrt(D)
        return {'initial_state': jax.random.normal(k0, (B, D), jnp.float32), 'inputs': jax.random.normal(k1, (B, T, D), jnp.float32), 'W_ih': jax.random.normal(k2, (D, 3 * D), jnp.float32) * scale, 'W_hh': jax.random.normal(k3, (D, 3 * D), jnp.float32) * scale, 'b_ih': jnp.zeros((3 * D,), jnp.float32), 'b_hh': jnp.zeros((3 * D,), jnp.float32)}
    _L0_cond_all = _L0_cond_setup()
    _L0_cond_in = {k: v for k, v in _L0_cond_all.items() if k in ('W_ih', 'W_hh', 'b_ih', 'b_hh')}
    del _L0_cond_all

    def _L0_ffn_setup():
        import jax, jax.numpy as jnp
        import numpy as np
        TOP_K = 2
        key = jax.random.key(seed)
        ks = jax.random.split(key, 5)
        B, T, D, E, H = (4, 512, 512, 8, 352)
        s = 1.0 / np.sqrt(D)
        sh = 1.0 / np.sqrt(H)
        return {'x': jax.random.normal(ks[0], (B, T, D), dtype=jnp.float32), 'Wg': jax.random.normal(ks[1], (E, D), dtype=jnp.float32) * s, 'W1': jax.random.normal(ks[2], (E, H, D), dtype=jnp.float32) * s, 'W2': jax.random.normal(ks[3], (E, H, D), dtype=jnp.float32) * s, 'W3': jax.random.normal(ks[4], (E, D, H), dtype=jnp.float32) * sh}
    _L0_ffn_all = _L0_ffn_setup()
    _L0_ffn_in = {k: v for k, v in _L0_ffn_all.items() if k in ('Wg', 'W1', 'W2', 'W3')}
    del _L0_ffn_all
    return {'x': x, 'cond_2048': cond_2048, 'L0_cond_W_ih': _L0_cond_in['W_ih'], 'L0_cond_W_hh': _L0_cond_in['W_hh'], 'L0_cond_b_ih': _L0_cond_in['b_ih'], 'L0_cond_b_hh': _L0_cond_in['b_hh'], 'L0_ffn_Wg': _L0_ffn_in['Wg'], 'L0_ffn_W1': _L0_ffn_in['W1'], 'L0_ffn_W2': _L0_ffn_in['W2'], 'L0_ffn_W3': _L0_ffn_in['W3']}

def reference(x, cond_2048, L0_cond_W_ih, L0_cond_W_hh, L0_cond_b_ih, L0_cond_b_hh, L0_ffn_Wg, L0_ffn_W1, L0_ffn_W2, L0_ffn_W3):
    import jax
    import jax.numpy as jnp

    def _L0_cond_ref(initial_state, inputs, W_ih, W_hh, b_ih, b_hh):
        import jax, jax.numpy as jnp
        import numpy as np
        B, T, D = (16, 128, 512)
        "ScanOverTime(GRU cell): sequential per-timestep module call with\n            dict-state passing; merge_dict_trees stacks the per-step\n            'state_predicted' tensors along axis=1 -> [B, T, D]."

        def cell(h, x):
            gi = x @ W_ih + b_ih
            gh = h @ W_hh + b_hh
            i_r, i_z, i_n = jnp.split(gi, 3, axis=-1)
            h_r, h_z, h_n = jnp.split(gh, 3, axis=-1)
            r = jax.nn.sigmoid(i_r + h_r)
            z = jax.nn.sigmoid(i_z + h_z)
            n = jnp.tanh(i_n + r * h_n)
            h_new = (1.0 - z) * n + z * h
            return (h_new, h_new)
        xs = jnp.swapaxes(inputs, 0, 1)
        _, hs = jax.lax.scan(cell, initial_state, xs)
        return jnp.swapaxes(hs, 0, 1)

    def _L0_ffn_ref(x, Wg, W1, W2, W3):
        import jax, jax.numpy as jnp
        import numpy as np
        TOP_K = 2
        E = Wg.shape[0]
        scores = jnp.einsum('btd,ed->bte', x, Wg)
        topk_s, topk_i = jax.lax.top_k(scores, TOP_K)
        probs = jax.nn.softmax(topk_s, axis=-1)
        onehot = (topk_i[..., None] == jnp.arange(E)).astype(x.dtype)
        w = jnp.einsum('btk,btke->bte', probs, onehot)
        y = jnp.zeros_like(x)
        for e in range(E):
            h = jax.nn.silu(jnp.einsum('btd,hd->bth', x, W1[e])) * jnp.einsum('btd,hd->bth', x, W2[e])
            y = y + w[..., e:e + 1] * jnp.einsum('bth,dh->btd', h, W3[e])
        return y
    x = x + _L0_ffn_ref(_L0_cond_ref(cond_2048, x, L0_cond_W_ih, L0_cond_W_hh, L0_cond_b_ih, L0_cond_b_hh), L0_ffn_Wg, L0_ffn_W1, L0_ffn_W2, L0_ffn_W3)
    return x

_drawn_inputs = setup_inputs


def setup_inputs(seed=0):
    import zlib

    import numpy as np

    out = dict(_drawn_inputs(seed))
    spreads = {'L0_cond_b_ih': (0.0, 0.1), 'L0_cond_b_hh': (0.0, 0.323)}
    factors = {'cond_2048': 3.616}
    for name, (base, spread) in spreads.items():
        noise = np.random.default_rng([zlib.crc32(name.encode()), seed]).standard_normal(out[name].shape)
        drawn = base * np.exp(spread * noise) if base else spread * noise
        out[name] = jnp.asarray(drawn.astype(out[name].dtype))
    for name, factor in factors.items():
        out[name] = (out[name] * factor).astype(out[name].dtype)
    return out
```

```python
from contextlib import ExitStack

import concourse.bass as bass
from concourse import mybir

F32 = mybir.dt.float32
F32R = mybir.dt.float32r
F16 = mybir.dt.float16
I32 = mybir.dt.int32
U32 = mybir.dt.uint32
ALU = mybir.AluOpType
ACT = mybir.ActivationFunctionType
AX_X = mybir.AxisListType.X
AX_XY = mybir.AxisListType.XY
RMAX = bass.bass_isa.ReduceOp.max

P = 128


def gru_moe_kernel(nc, x_feat, x_tok, h0_feat, w_hh, b_feat, w_gate, w_units, w_inproj, out):
    CHUNKS, _, K, TOK = x_feat.shape
    B = h0_feat.shape[2]
    D = K * P
    M = 3 * K
    E = w_gate.shape[2]
    UNITS = w_units.shape[0]
    PER_E = UNITS // E
    GROUPS = w_inproj.shape[0]
    STEPS = TOK // B
    GS = STEPS // GROUPS
    UG = UNITS // GROUPS
    MG = M // GROUPS
    TT = TOK // P
    W1, W2, W3 = 0, K * P, 2 * K * P
    UCOLS = 3 * K * P
    SPLITS = 3
    assert UG % SPLITS == 0 and UG % 2 == 0 and MG * K * P == UCOLS

    BLOCKS = [
        [("A", 0), ("B", 0), ("G", 0)],
        [("A", 1), ("B", 1), ("Y", 0)],
        [("A", 2), ("B", 2)],
        [("Y", 1), ("A", 3), ("B", 3)],
        [("G", 1), ("Y", 2), ("A", 4)],
        [("B", 4), ("Y", 3)],
        [("A", 5), ("B", 5), ("Y", 4)],
        [("G", 2), ("Y", 5)],
    ]
    assert GS == len(BLOCKS)

    (RZ_A, RZ_B, HN_A, HN_B, R_HN, N_PRE, Z_H, ONE_Z, N_MIX, H_NEW, H_HI, H_LO, H_LOG) = range(1, 14)
    GRU_OPS = 13
    (SILU, GATED, WEIGHTED, HID_LO) = range(1, 5)
    FFN_OPS = 4

    with ExitStack() as ctx:
        def sb(name, shape, dt=F32):
            return ctx.enter_context(nc.sbuf_tensor(name, shape, dt))

        def ps(name, shape):
            return ctx.enter_context(nc.psum_tensor(name, shape, F32))

        def sem(name):
            return ctx.enter_context(nc.semaphore(name))

        ident = sb("ident", [P, P])
        iota_e = sb("iota_e", [P, E])
        zeros_r = sb("zeros_r", [P, P], F32R)
        whh = sb("whh", [P, 2, K, M * P], F16)
        bias = sb("bias", [P, 2, M])
        gi_bias = sb("gi_bias", [P, M])
        bhn = sb("bhn", [P, K, B])
        wg_raw = sb("wg_raw", [P, K, E])
        wg = sb("wg", [P, K, P], F32R)
        mags = sb("mags", [P, 8])
        spare = sb("spare", [P, 1])
        sc = sb("sc", [P, 8])
        h_now = sb("h_now", [P, 2, K, B])
        h_parts = sb("h_parts", [P, K, 2, B], F16)
        h_log = sb("h_log", [P, K, TOK])
        rz1 = sb("rz1", [P, 2 * K, B])
        rz = sb("rz", [P, 2 * K, B])
        rzs = sb("rzs", [P, 2 * K, B])
        hn1 = sb("hn1", [P, K, B])
        hn = sb("hn", [P, K, B])
        rh = sb("rh", [P, K, B])
        npre = sb("npre", [P, K, B])
        nt = sb("nt", [P, K, B])
        zh = sb("zh", [P, K, B])
        omz = sb("omz", [P, K, B])
        nmix = sb("nmix", [P, K, B])
        x_raw = sb("x_raw", [P, K, TOK])
        x_split = sb("x_split", [P, 2, K, TOK], F32R)
        wi_split = sb("wi_split", [P, 2, UCOLS], F32R)
        gi = sb("gi", [P, 2, M, TOK])
        assert M * TOK == K * M * P
        whh_raw = gi[:, 1].rearrange("p a b -> p (a b)").rearrange("p (k m) -> p k m", k=K)
        f_split = sb("f_split", [P, 2, K, TOK], F32R)
        w_raw = sb("w_raw", [P, UCOLS])
        wu_split = sb("wu_split", [P, SPLITS, 2, UCOLS], F32R)
        sig = sb("sig", [P, TOK])
        hid = sb("hid", [P, TOK])
        hid_split = sb("hid_split", [P, 2, 2, TOK], F32R)
        scT = sb("scT", [2 * E, TOK])
        score = sb("score", [P, TT, E])
        score1 = sb("score1", [P, TT, E])
        top = sb("top", [P, TT, 8])
        top_i = sb("top_i", [P, TT, 8], U32)
        top_f = sb("top_f", [P, TT, 8])
        gap = sb("gap", [P, TT])
        prob = sb("prob", [P, 2, TT])
        w_1 = sb("w_1", [P, TT, E])
        w_2 = sb("w_2", [P, TT, E])
        w_te = sb("w_te", [P, TT, E])
        wT = sb("wT", [E, TOK])
        w_exp = sb("w_exp", [P, 2, TOK])
        y_sb = sb("y_sb", [P, TT, D])
        w_dram = nc.dram_tensor("w_scratch", [E, TOK], F32, kind="Internal").ap()

        y_ps = ps("y_ps", [P, TT, 512])
        a_ps = ps("a_ps", [P, 512])
        b_ps = ps("b_ps", [P, 512])
        gh_ps = ps("gh_ps", [P, M, 2, B])
        misc_ps = ps("misc_ps", [P, 512])

        loaded = sem("loaded")
        const_ready = sem("const_ready")
        setup = sem("setup")
        mag_ready = sem("mag_ready")
        gh_ready = sem("gh_ready")
        gru_ops = sem("gru_ops")
        sig_rz = sem("sig_rz")
        tanh_n = sem("tanh_n")
        x_loaded = sem("x_loaded")
        x_hi = sem("x_hi")
        x_lo = sem("x_lo")
        wi_loaded = sem("wi_loaded")
        wi_hi = sem("wi_hi")
        wi_lo = sem("wi_lo")
        gi_mm = sem("gi_mm")
        gi_ready = sem("gi_ready")
        wu_loaded = sem("wu_loaded")
        wu_hi = sem("wu_hi")
        wu_lo = sem("wu_lo")
        wu_used = sem("wu_used")
        a_mm = sem("a_mm")
        b_mm = sem("b_mm")
        sig_a = sem("sig_a")
        ffn_ops = sem("ffn_ops")
        hid_hi = sem("hid_hi")
        f_hi = sem("f_hi")
        f_lo = sem("f_lo")
        score_mm = sem("score_mm")
        route_ops = sem("route_ops")
        score_T = sem("score_T")
        probs = sem("probs")
        w_T = sem("w_T")
        wT_out = sem("wT_out")
        w_loaded = [sem("w_even_loaded"), sem("w_odd_loaded")]
        y_read = sem("y_read")
        xres_loaded = sem("xres_loaded")
        stored = sem("stored")

        SC_W, SC_H, SC_INV, SC_IH, SC_NH, SC_PW, SC_PH = range(7)

        def scale(i):
            return sc[:, i:i + 1]

        def walk(eng, start, group, finish):
            with eng.Fori(0, GROUPS) as g:
                group(-1, g, False, True, False)
            start(0, True, False)
            with eng.Fori(0, GROUPS) as g:
                group(0, g, True, True, False)
            with eng.Fori(1, CHUNKS - 1) as c:
                start(c, True, True)
                with eng.Fori(0, GROUPS) as g:
                    group(c, g, True, True, True)
                finish(c)
            start(CHUNKS - 1, False, True)
            with eng.Fori(0, GROUPS) as g:
                group(CHUNKS - 1, g, True, False, True)
            finish(CHUNKS - 1)
            start(CHUNKS, False, True)
            with eng.Fori(0, GROUPS) as g:
                group(CHUNKS, g, False, False, True)
            finish(CHUNKS)

        def step_no(c, g, s):
            return c * STEPS + g * GS + s

        def unit_no(c, g, u):
            return (c - 1) * UNITS + g * UG + u

        def piece_no(c, g, j):
            return (c + 1) * M + g * MG + j

        def group_no(c, g):
            return (c + 1) * GROUPS + g

        N_ROUTE = 6 + 2 * TT + 3 * TT
        N_SETUP = 20 + E

        def settle(eng):
            if eng is nc.sync:
                eng.wait_ge(const_ready, 2)
            else:
                nc.vector.memset(spare[:], 0.0)

        block = ctx.enter_context(nc.Block())

        @block.sync
        def _(sp):
            sp.dma_start(whh_raw[:], w_hh).then_inc(loaded, 16)
            sp.dma_start(h_now[:, 1], h0_feat).then_inc(loaded, 16)
            sp.dma_start(bias[:], b_feat).then_inc(loaded, 16)
            sp.dma_start(wg_raw[:], w_gate).then_inc(loaded, 16)

            def load_x(n):
                settle(nc.sync)
                sp.wait_ge(x_lo, n)
                sp.dma_start(x_raw[:], x_feat[bass.ds(n, 1)].rearrange("o p k t -> (o p) k t")
                             ).then_inc(x_loaded, 16)

            def start(c, proj, ffn):
                if proj:
                    load_x(c + 1)

            def group(c, g, rec, proj, ffn):
                if proj:
                    settle(nc.sync)
                    sp.wait_ge(wi_lo, group_no(c, g))
                    if ffn:
                        settle(nc.sync)
                        sp.wait_ge(wu_lo, unit_no(c, g, 0))
                    sp.dma_start(w_raw[:], w_inproj[bass.ds(g, 1)].rearrange("o p n -> (o p) n")
                                 ).then_inc(wi_loaded, 16)
                if ffn:
                    for u in range(UG):
                        n = unit_no(c, g, u)
                        settle(nc.sync)
                        sp.wait_ge(wu_lo, n)
                        if proj and u == 0:
                            settle(nc.sync)
                            sp.wait_ge(wi_lo, group_no(c, g) + 1)
                        sp.dma_start(w_raw[:],
                                     w_units[bass.ds(g * UG + u, 1)].rearrange("o p n -> (o p) n")
                                     ).then_inc(wu_loaded, 16)

            load_x(0)
            walk(sp, start, group, lambda c: None)

        @block.gpsimd
        def _(pool):
            nc.gpsimd.memset(ident[:], 0.0).then_inc(const_ready, 1)
            pool.wait_ge(const_ready, 1)
            nc.gpsimd.affine_select(out=ident[:], in_=ident[:], compare_op=ALU.not_equal, fill=1.0,
                                    base=0, pattern=[[-1, P]], channel_multiplier=1
                                    ).then_inc(const_ready, 1)
            pool.wait_ge(const_ready, 2)
            pool.wait_ge(setup, 3)
            nc.gpsimd.partition_all_reduce(mags[:, 4:5], mags[:, 2:3], P, RMAX).then_inc(mag_ready, 1)
            nc.gpsimd.partition_all_reduce(mags[:, 5:6], mags[:, 3:4], P, RMAX).then_inc(mag_ready, 1)

            for f in range(CHUNKS):
                if f:
                    pool.wait_ge(stored, 16 * f)
                pool.dma_start(y_sb[:], x_tok[bass.ds(f * TOK, TOK), :].rearrange(
                    "(t p) d -> p t d", p=P)).then_inc(xres_loaded, 16)
                pool.wait_ge(route_ops, N_ROUTE * (f + 1))
                if f:
                    for e in range(2):
                        pool.wait_ge(w_loaded[e], 16 * (E // 2) * f)
                pool.dma_start(w_dram, wT[:]).then_inc(wT_out, 16)
                pool.wait_ge(wT_out, 16 * (f + 1))
                for e in range(E):
                    n = f * UNITS + (e - 1) * PER_E
                    if e == 0:
                        pool.wait_ge(ffn_ops, FFN_OPS * (f * UNITS + 1))
                    if e > 1:
                        pool.wait_ge(ffn_ops, FFN_OPS * (n + 1))
                    pool.dma_start(w_exp[:, e % 2], w_dram[e:e + 1, :].to_broadcast([P, TOK])
                                   ).then_inc(w_loaded[e % 2], 16)
                pool.wait_ge(y_read, TT * (f + 1))
                pool.dma_start(out[bass.ds(f * TOK, TOK), :].rearrange("(t p) d -> p t d", p=P),
                               y_sb[:]).then_inc(stored, 16)
            pool.wait_ge(stored, 16 * CHUNKS)

        @block.scalar
        def _(act):
            def start(c, proj, ffn):
                if proj:
                    split_x(c + 1)
                if ffn:
                    f = c - 1
                    act.wait_ge(gru_ops, GRU_OPS * STEPS * c)
                    act.wait_ge(b_mm, UNITS * f)
                    nc.scalar.copy(f_split[:, 0], h_log[:]).then_inc(f_hi, 1)
                    act.wait_ge(route_ops, (N_ROUTE) * f + N_ROUTE - 3 * TT - 1)
                    nc.scalar.activation(prob[:, 0], gap[:], ACT.Sigmoid).then_inc(probs, 1)
                    nc.scalar.activation(prob[:, 1], gap[:], ACT.Sigmoid, scale=-1.0).then_inc(probs, 1)

            def split_x(n):
                act.wait_ge(x_loaded, 16 * (n + 1))
                act.wait_ge(gi_mm, M * n)
                nc.scalar.copy(x_split[:, 0], x_raw[:]).then_inc(x_hi, 1)

            def split_wi(c, g):
                act.wait_ge(wi_loaded, 16 * (group_no(c, g) + 1))
                act.wait_ge(gi_mm, piece_no(c, g, 0))
                nc.scalar.copy(wi_split[:, 0], w_raw[:]).then_inc(wi_hi, 1)

            def split_wu(c, g, u):
                n = unit_no(c, g, u)
                act.wait_ge(wu_loaded, 16 * (n + 1))
                act.wait_ge(wu_used, n + 1)
                nc.scalar.copy(wu_split[:, u % SPLITS, 0], w_raw[:]).then_inc(wu_hi, 1)

            def group(c, g, rec, proj, ffn):
                if proj:
                    split_wi(c, g)
                if ffn:
                    split_wu(c, g, 0)
                for s in range(GS):
                    if rec:
                        t = step_no(c, g, s)
                        act.wait_ge(gru_ops, GRU_OPS * t + RZ_B)
                        nc.scalar.activation(rzs[:], rz[:], ACT.Sigmoid).then_inc(sig_rz, 1)
                        act.wait_ge(gru_ops, GRU_OPS * t + N_PRE)
                        nc.scalar.activation(nt[:], npre[:], ACT.Tanh).then_inc(tanh_n, 1)
                    for kind, i in BLOCKS[s]:
                        if kind == "G" and proj:
                            n = piece_no(c, g, i)
                            act.wait_ge(gi_mm, n + 1)
                            nc.scalar.activation(gi[:, bass.ds((c + 1) % 2, 1), bass.ds(g * MG + i, 1), :],
                                                 misc_ps[:], ACT.Identity,
                                                 bias=gi_bias[:, bass.ds(g * MG + i, 1)]
                                                 ).then_inc(gi_ready, 1)
                        if kind == "A" and ffn:
                            n = unit_no(c, g, i)
                            act.wait_ge(a_mm, n + 1)
                            nc.scalar.activation(sig[:], a_ps[:], ACT.Sigmoid, scale=scale(SC_IH)
                                                 ).then_inc(sig_a, 1)
                            if i + 1 < UG:
                                split_wu(c, g, i + 1)
                        if kind == "B" and ffn:
                            n = unit_no(c, g, i)
                            act.wait_ge(ffn_ops, FFN_OPS * (n + 1) + WEIGHTED)
                            act.wait_ge(wu_used, n + 2)
                            nc.scalar.copy(hid_split[:, i % 2, 0], hid[:]).then_inc(hid_hi, 1)

            act.wait_ge(setup, N_SETUP)
            split_x(0)
            walk(act, start, group, lambda c: None)

        @block.vector
        def _(dve):
            done = [0]

            def chain(ins):
                done[0] += 1
                ins.then_inc(setup, 1)
                dve.wait_ge(setup, done[0])

            V = nc.vector
            dve.sem_inc(ffn_ops, FFN_OPS)
            dve.wait_ge(loaded, 64)
            chain(V.tensor_reduce(mags[:, 2:3], whh_raw[:], AX_XY, ALU.max, apply_absolute_value=True))
            chain(V.tensor_reduce(mags[:, 3:4], h_now[:, 1], AX_XY, ALU.max, apply_absolute_value=True))
            chain(V.tensor_scalar(mags[:, 3:4], mags[:, 3:4], 1.0, None, ALU.max))
            dve.wait_ge(mag_ready, 2)
            chain(V.tensor_scalar(mags[:, 4:6], mags[:, 4:6], 2.0 ** -40, None, ALU.max))
            chain(V.tensor_scalar(sc[:, SC_PW:SC_PH + 1].bitcast(I32), mags[:, 4:6].bitcast(I32),
                                  0x7F800000, None, ALU.bitwise_and))
            chain(V.tensor_scalar(sc[:, SC_W:SC_H + 1].bitcast(I32), sc[:, SC_PW:SC_PH + 1].bitcast(I32),
                                  -1.0, float((127 + 14 + 127) << 23), ALU.mult, ALU.add))
            chain(V.tensor_scalar(sc[:, SC_IH:SC_IH + 1], scale(SC_PH), 2.0 ** -14, None, ALU.mult))
            chain(V.tensor_scalar(sc[:, SC_INV:SC_INV + 1], scale(SC_PW), 2.0 ** -14, scale(SC_IH),
                                  ALU.mult, ALU.mult))
            chain(V.tensor_scalar(sc[:, SC_NH:SC_NH + 1], scale(SC_H), -1.0, None, ALU.mult))
            chain(V.tensor_scalar(whh[:, 0], whh_raw[:], scale(SC_W), None, ALU.mult))
            chain(V.scalar_tensor_tensor(out=whh[:, 1], in0=whh_raw[:], scalar=scale(SC_W),
                                         in1=whh[:, 0], op0=ALU.mult, op1=ALU.subtract))
            chain(V.tensor_scalar(h_now[:, 0], h_now[:, 1], scale(SC_H), None, ALU.mult))
            chain(V.tensor_copy(h_parts[:, :, 0], h_now[:, 0]))
            chain(V.tensor_tensor(h_parts[:, :, 1], h_now[:, 0], h_parts[:, :, 0], ALU.subtract))
            chain(V.tensor_copy(gi_bias[:], bias[:, 0]))
            chain(V.tensor_tensor(gi_bias[:, 0:2 * K], bias[:, 0, 0:2 * K], bias[:, 1, 0:2 * K], ALU.add))
            chain(V.tensor_copy(bhn[:], bias[:, 1, 2 * K:M].unsqueeze(2).to_broadcast([P, K, B])))
            chain(V.memset(zeros_r[:].bitcast(F32), 0.0))
            for k in range(K):
                V.tensor_copy(wg[:, k], zeros_r[:].bitcast(F32))
            for e in range(E):
                chain(V.memset(iota_e[:, e:e + 1], float(e)))
            chain(V.tensor_copy(wg[:, :, 0:E], wg_raw[:]))
            chain(V.tensor_tensor(wg[:, :, E:2 * E], wg_raw[:], wg[:, :, 0:E].bitcast(F32), ALU.subtract))
            assert done[0] == N_SETUP, done[0]

            def split_x(n):
                dve.wait_ge(x_hi, n + 1)
                V.tensor_tensor(x_split[:, 1], x_raw[:], x_split[:, 0].bitcast(F32), ALU.subtract
                                ).then_inc(x_lo, 1)

            def split_wi(c, g):
                dve.wait_ge(wi_hi, group_no(c, g) + 1)
                V.tensor_tensor(wi_split[:, 1], w_raw[:], wi_split[:, 0].bitcast(F32), ALU.subtract
                                ).then_inc(wi_lo, 1)

            def split_wu(c, g, u):
                dve.wait_ge(wu_hi, unit_no(c, g, u) + 1)
                V.tensor_tensor(wu_split[:, u % SPLITS, 1], w_raw[:],
                                wu_split[:, u % SPLITS, 0].bitcast(F32), ALU.subtract
                                ).then_inc(wu_lo, 1)

            def route(f):
                base = N_ROUTE * f
                n = [0]

                def op(ins, wait=True):
                    ins.then_inc(route_ops, 1)
                    n[0] += 1
                    if wait:
                        dve.wait_ge(route_ops, base + n[0])

                dve.wait_ge(score_mm, f + 1)
                op(V.tensor_copy(scT[:], misc_ps[0:2 * E, :]), False)
                dve.wait_ge(score_T, f + 1)
                halves = misc_ps[:, 0:TT * 2 * E].rearrange("p (t e) -> p t e", t=TT)
                op(V.tensor_scalar(score1[:], halves[:, :, 0:E], scale(SC_IH), None, ALU.mult))
                op(V.scalar_tensor_tensor(out=score[:], in0=halves[:, :, E:2 * E], scalar=scale(SC_IH),
                                          in1=score1[:], op0=ALU.mult, op1=ALU.add))
                settle(nc.vector)
                for t in range(TT):
                    op(V.max(top[:, t], score[:, t]), t == TT - 1)
                settle(nc.vector)
                for t in range(TT):
                    op(V.max_index(top_i[:, t], top[:, t], score[:, t]), t == TT - 1)
                op(V.tensor_copy(top_f[:], top_i[:]))
                op(V.tensor_tensor(gap[:], top[:, :, 0], top[:, :, 1], ALU.subtract))
                dve.wait_ge(probs, 2 * (f + 1))
                for t in range(TT):
                    op(V.tensor_scalar(w_1[:, t], iota_e[:], top_f[:, t, 0:1], prob[:, 0, t:t + 1],
                                       ALU.is_equal, ALU.mult), False)
                for t in range(TT):
                    op(V.tensor_scalar(w_2[:, t], iota_e[:], top_f[:, t, 1:2], prob[:, 1, t:t + 1],
                                       ALU.is_equal, ALU.mult), t == TT - 1)
                for t in range(TT):
                    op(V.tensor_tensor(w_te[:, t], w_1[:, t], w_2[:, t], ALU.add), False)
                dve.wait_ge(w_T, f + 1)
                dve.wait_ge(wT_out, 16 * f)
                op(V.tensor_copy(wT[:], misc_ps[0:E, :]), False)
                assert n[0] == N_ROUTE, n[0]

            def start(c, proj, ffn):
                if proj:
                    split_x(c + 1)
                if ffn:
                    f = c - 1
                    dve.wait_ge(f_hi, f + 1)
                    V.tensor_tensor(f_split[:, 1], h_log[:], f_split[:, 0].bitcast(F32), ALU.subtract
                                    ).then_inc(f_lo, 1)
                    route(f)

            def gru_step(c, g, s):
                t = step_no(c, g, s)
                now, new = s % 2, (s + 1) % 2
                at = g * (GS * B) + s * B
                gi_c = gi[:, bass.ds(c % 2, 1), :, bass.ds(at, B)].rearrange("p o m b -> p (o m) b")
                inv = scale(SC_INV)

                def after(k):
                    dve.wait_ge(gru_ops, GRU_OPS * t + k)

                def op(ins):
                    ins.then_inc(gru_ops, 1)

                if s == 0:
                    dve.wait_ge(gi_ready, M * (c + 1))
                dve.wait_ge(gh_ready, t + 1)
                op(V.scalar_tensor_tensor(out=rz1[:], in0=gh_ps[:, 0:2 * K, 0, :], scalar=inv,
                                          in1=gi_c[:, 0:2 * K], op0=ALU.mult, op1=ALU.add))
                after(RZ_A)
                op(V.scalar_tensor_tensor(out=rz[:], in0=gh_ps[:, 0:2 * K, 1, :], scalar=inv,
                                          in1=rz1[:], op0=ALU.mult, op1=ALU.add))
                op(V.scalar_tensor_tensor(out=hn1[:], in0=gh_ps[:, 2 * K:M, 0, :], scalar=inv,
                                          in1=bhn[:], op0=ALU.mult, op1=ALU.add))
                after(HN_A)
                op(V.scalar_tensor_tensor(out=hn[:], in0=gh_ps[:, 2 * K:M, 1, :], scalar=inv,
                                          in1=hn1[:], op0=ALU.mult, op1=ALU.add))
                after(HN_B)
                dve.wait_ge(sig_rz, t + 1)
                op(V.tensor_tensor(rh[:], rzs[:, 0:K], hn[:], ALU.mult))
                after(R_HN)
                op(V.tensor_tensor(npre[:], rh[:], gi_c[:, 2 * K:M], ALU.add))
                op(V.tensor_tensor(zh[:], rzs[:, K:2 * K], h_now[:, now], ALU.mult))
                op(V.tensor_scalar(omz[:], rzs[:, K:2 * K], scale(SC_NH), scale(SC_H), ALU.mult, ALU.add))
                after(ONE_Z)
                dve.wait_ge(tanh_n, t + 1)
                op(V.tensor_tensor(nmix[:], nt[:], omz[:], ALU.mult))
                after(N_MIX)
                op(V.tensor_tensor(h_now[:, new], nmix[:], zh[:], ALU.add))
                after(H_NEW)
                op(V.tensor_copy(h_parts[:, :, 0], h_now[:, new]))
                after(H_HI)
                op(V.tensor_tensor(h_parts[:, :, 1], h_now[:, new], h_parts[:, :, 0], ALU.subtract))
                op(V.tensor_copy(h_log[:, :, bass.ds(at, B)], h_now[:, new]))

            def group(c, g, rec, proj, ffn):
                if proj:
                    split_wi(c, g)
                if ffn:
                    split_wu(c, g, 0)
                for s in range(GS):
                    if rec:
                        gru_step(c, g, s)
                    for kind, i in BLOCKS[s] if ffn else []:
                        n = unit_no(c, g, i)
                        if kind == "A":
                            dve.wait_ge(sig_a, n + 1)
                            dve.wait_ge(ffn_ops, FFN_OPS * (n + 1))
                            V.scalar_tensor_tensor(out=hid[:], in0=a_ps[:], scalar=scale(SC_IH),
                                                   in1=sig[:], op0=ALU.mult, op1=ALU.mult
                                                   ).then_inc(ffn_ops, 1)
                            if i + 1 < UG:
                                split_wu(c, g, i + 1)
                        if kind == "B":
                            at = FFN_OPS * (n + 1)
                            dve.wait_ge(b_mm, n + 1)
                            dve.wait_ge(ffn_ops, at + SILU)
                            V.scalar_tensor_tensor(out=hid[:], in0=b_ps[:], scalar=scale(SC_IH),
                                                   in1=hid[:], op0=ALU.mult, op1=ALU.mult
                                                   ).then_inc(ffn_ops, 1)
                            e = i // PER_E
                            if i % PER_E == 0:
                                dve.wait_ge(w_loaded[e], 16 * ((c - 1) * (E // 2) + g + 1))
                            dve.wait_ge(ffn_ops, at + GATED)
                            V.tensor_tensor(hid[:], hid[:], w_exp[:, e],
                                            ALU.mult).then_inc(ffn_ops, 1)
                            dve.wait_ge(hid_hi, n + 1)
                            V.tensor_tensor(hid_split[:, i % 2, 1], hid[:],
                                            hid_split[:, i % 2, 0].bitcast(F32), ALU.subtract
                                            ).then_inc(ffn_ops, 1)

            def finish(c):
                f = c - 1
                dve.wait_ge(wu_used, SPLITS + UNITS * (f + 1))
                dve.wait_ge(xres_loaded, 16 * (f + 1))
                for t in range(TT):
                    V.tensor_tensor(y_sb[:, t], y_ps[:, t], y_sb[:, t], ALU.add).then_inc(y_read, 1)

            split_x(0)
            walk(dve, start, group, finish)

        @block.tensor
        def _(pe):
            PARTS = ((0, 0), (0, 1), (1, 0))
            pe.sem_inc(wu_used, SPLITS)

            def recur(c, g, s):
                t = step_no(c, g, s)
                pe.wait_ge(gru_ops, GRU_OPS * t)
                for m in range(M):
                    for k in range(K):
                        for part in range(2):
                            mm = pe.matmul(gh_ps[:, m].rearrange("p a b -> p (a b)"),
                                           whh[:, part, k, m * P:(m + 1) * P],
                                           h_parts[:, k].rearrange("p a b -> p (a b)"),
                                           start=(k == 0 and part == 0), stop=(k == K - 1 and part == 1))
                mm.then_inc(gh_ready, 1)

            def project(c, g, j):
                n = piece_no(c, g, j)
                if j == 0:
                    pe.wait_ge(x_lo, c + 2)
                    pe.wait_ge(wi_lo, group_no(c, g) + 1)
                pe.wait_ge(gi_ready, n)
                for i, (a, b) in enumerate(PARTS):
                    for k in range(K):
                        mm = pe.matmul(misc_ps[:], wi_split[:, a, (j * K + k) * P:(j * K + k + 1) * P],
                                       x_split[:, b, k], start=(i == 0 and k == 0),
                                       stop=(i == 2 and k == K - 1))
                mm.then_inc(gi_mm, 1)

            def up(c, g, u, dst, col, signal):
                n = unit_no(c, g, u)
                if signal is a_mm:
                    pe.wait_ge(wu_lo, n + 1)
                    pe.wait_ge(ffn_ops, FFN_OPS * n + SILU)
                else:
                    pe.wait_ge(ffn_ops, FFN_OPS * n + GATED)
                for i, (a, b) in enumerate(PARTS):
                    for k in range(K):
                        mm = pe.matmul(dst[:], wu_split[:, u % SPLITS, a, col + k * P:col + (k + 1) * P],
                                       f_split[:, b, k], start=(i == 0 and k == 0),
                                       stop=(i == 2 and k == K - 1))
                mm.then_inc(signal, 1)

            def down(c, g, u):
                n = unit_no(c, g, u)
                pe.wait_ge(ffn_ops, FFN_OPS * (n + 1) + HID_LO)
                for t in range(TT):
                    for a, b in PARTS:
                        mm = pe.matmul(y_ps[:, t], hid_split[:, u % 2, a, t * P:(t + 1) * P],
                                       wu_split[:, u % SPLITS, b, W3:W3 + D],
                                       start=False, stop=True, skip_group_check=True)
                mm.then_inc(wu_used, 1)

            def start(c, proj, ffn):
                if not ffn:
                    return
                f = c - 1
                pe.wait_ge(y_read, TT * f)
                for t in range(TT):
                    pe.matmul(y_ps[:, t], zeros_r[:], wg[:].rearrange("p k n -> p (k n)"), start=True, stop=True,
                              skip_group_check=True)
                pe.wait_ge(f_lo, f + 1)
                pe.wait_ge(gi_ready, M * (c + 1) if not isinstance(c, int) or c < CHUNKS else M * CHUNKS)
                for b in range(2):
                    for k in range(K):
                        mm = pe.matmul(misc_ps[:], wg[:, k], f_split[:, b, k],
                                       start=(b == 0 and k == 0), stop=(b == 1 and k == K - 1))
                mm.then_inc(score_mm, 1)
                pe.wait_ge(route_ops, N_ROUTE * f + 1)
                for t in range(TT):
                    mm = pe.matmul(misc_ps[:, t * 2 * E:(t + 1) * 2 * E], scT[:, t * P:(t + 1) * P],
                                      ident[0:2 * E, 0:2 * E])
                mm.then_inc(score_T, 1)
                pe.wait_ge(route_ops, N_ROUTE * (f + 1) - 1)
                for t in range(TT):
                    mm = pe.matmul(misc_ps[0:E, t * P:(t + 1) * P], w_te[:, t], ident[:])
                mm.then_inc(w_T, 1)

            def group(c, g, rec, proj, ffn):
                for s in range(GS):
                    if rec:
                        recur(c, g, s)
                    for kind, i in BLOCKS[s]:
                        if kind == "G" and proj:
                            project(c, g, i)
                        elif kind == "A" and ffn:
                            up(c, g, i, a_ps, W1, a_mm)
                        elif kind == "B" and ffn:
                            up(c, g, i, b_ps, W2, b_mm)
                        elif kind == "Y" and ffn:
                            down(c, g, i)

            pe.wait_ge(setup, N_SETUP)
            pe.wait_ge(const_ready, 2)
            walk(pe, start, group, lambda c: None)


def kernel(x, cond_2048, L0_cond_W_ih, L0_cond_W_hh, L0_cond_b_ih, L0_cond_b_hh,
           L0_ffn_Wg, L0_ffn_W1, L0_ffn_W2, L0_ffn_W3):
    import numpy as np
    import concourse.bacc as bacc
    from concourse import mybir as mb
    from concourse.bass_utils import run_bass_kernel_spmd

    x = np.asarray(x)
    B, T, D = x.shape
    K, M = D // P, 3 * D // P
    E, H, _ = np.asarray(L0_ffn_W1).shape
    STEPS, GROUPS = 32, 4
    CHUNKS, TOK = T // STEPS, STEPS * B
    HP = -(-H // P)

    x_tok = np.ascontiguousarray(x.transpose(1, 0, 2)).reshape(T * B, D)
    x_feat = np.ascontiguousarray(x_tok.reshape(CHUNKS, TOK, K, P).transpose(0, 3, 2, 1))

    def feat(w):
        return np.ascontiguousarray(w.reshape(K, P, -1).transpose(1, 0, 2))

    def padded(w):
        out = np.zeros((E, HP * P, D), w.dtype)
        out[:, :H] = w
        return out.reshape(E * HP, P, D)

    w1, w2 = padded(np.asarray(L0_ffn_W1)), padded(np.asarray(L0_ffn_W2))
    w3 = padded(np.asarray(L0_ffn_W3).transpose(0, 2, 1))

    def up_unit(w):
        return w.reshape(-1, P, K, P).transpose(0, 3, 2, 1).reshape(-1, P, K * P)

    w_units = np.ascontiguousarray(np.concatenate([up_unit(w1), up_unit(w2), w3], axis=2))
    w_ih = np.asarray(L0_cond_W_ih)
    w_inproj = np.ascontiguousarray(
        w_ih.reshape(K, P, GROUPS, M // GROUPS, P).transpose(2, 1, 3, 0, 4)).reshape(GROUPS, P, -1)
    b_feat = np.ascontiguousarray(
        np.stack([np.asarray(L0_cond_b_ih), np.asarray(L0_cond_b_hh)]).reshape(2, M, P).transpose(2, 0, 1))

    arrays = {
        "x_feat": x_feat,
        "x_tok": x_tok,
        "h0_feat": feat(np.asarray(cond_2048).T),
        "w_hh": feat(np.asarray(L0_cond_W_hh)),
        "b_feat": b_feat,
        "w_gate": feat(np.asarray(L0_ffn_Wg).T),
        "w_units": w_units,
        "w_inproj": w_inproj,
    }
    nc = bacc.Bacc("TRN2", target_bir_lowering=False, num_devices=1, dynamic_dma_scratch_size=8192)
    args = [nc.dram_tensor(f"in_{n}", a.shape, mb.dt.from_np(a.dtype), kind="ExternalInput").ap()
            for n, a in arrays.items()]
    y = nc.dram_tensor("out_y", (T * B, D), mb.dt.float32, kind="ExternalOutput").ap()
    gru_moe_kernel(nc, *args, y)
    r = run_bass_kernel_spmd(nc, [{f"in_{n}": a for n, a in arrays.items()}], core_ids=[0])
    return np.ascontiguousarray(r.results[0]["out_y"].reshape(T, B, D).transpose(1, 0, 2))
```

```python
from contextlib import ExitStack

import concourse.bass as bass
from concourse import mybir

F32 = mybir.dt.float32
F32R = mybir.dt.float32r
F16 = mybir.dt.float16
I32 = mybir.dt.int32
U32 = mybir.dt.uint32
ALU = mybir.AluOpType
ACT = mybir.ActivationFunctionType
AX_X = mybir.AxisListType.X
AX_XY = mybir.AxisListType.XY
RMAX = bass.bass_isa.ReduceOp.max

P = 128


def gru_moe_kernel(nc, x_feat, x_tok, h0_feat, w_hh, b_feat, w_gate, w_units, w_inproj, out):
    CHUNKS, _, K, TOK = x_feat.shape
    B = h0_feat.shape[2]
    D = K * P
    M = 3 * K
    E = w_gate.shape[2]
    UNITS = w_units.shape[0]
    GROUPS = 2
    STEPS = TOK // B
    GS = STEPS // GROUPS
    UG = UNITS // GROUPS
    EG = E // GROUPS
    HE = UNITS * P // E
    WI = w_inproj.shape[0]
    MW = M // WI
    assert WI == 2 + GROUPS and UG * P == EG * HE
    TT = TOK // P
    W1, W2, W3 = 0, K * P, 2 * K * P
    UCOLS = 3 * K * P
    SPLITS = 3
    assert MW * K * P == UCOLS and UG % 2 == 1 and EG % 2 == 0

    order = []
    for u in range(UG):
        order += [("A", u), ("B", u)] + [("Y", u - 1)] * (u > 0)
        order += [("G", (u - 4) // 3)] * (u in (4, 7))
    order += [("G", MW - 1), ("Y", UG - 1)]
    BLOCKS = [order[len(order) * s // GS:len(order) * (s + 1) // GS] for s in range(GS)]

    def experts_of(u):
        rows = []
        for e in range(u * P // HE, ((u + 1) * P - 1) // HE + 1):
            r0, r1 = max(0, e * HE - u * P), min(P, (e + 1) * HE - u * P)
            if r0 == 32 and r1 > 64:
                rows.append((e, r0, 64))
                r0 = 64
            rows.append((e, r0, r1))
        return rows

    (R_A, HN_A, R_B, HN_B, Z_A, R_HN, Z_B, N_PRE, Z_H, ONE_Z, N_MIX, H_HI, H_NEW, H_LO, H_LOG) = range(1, 16)
    GRU_OPS = 15
    (SILU, GATED, WEIGHTED, HID_LO) = range(1, 5)
    FFN_OPS = 4

    with ExitStack() as ctx:
        def sb(name, shape, dt=F32):
            return ctx.enter_context(nc.sbuf_tensor(name, shape, dt))

        def ps(name, shape):
            return ctx.enter_context(nc.psum_tensor(name, shape, F32))

        def sem(name):
            return ctx.enter_context(nc.semaphore(name))

        ident = sb("ident", [P, P])
        iota_e = sb("iota_e", [P, E])
        zeros_r = sb("zeros_r", [P, P], F32R)
        whh = sb("whh", [P, 2, K, M * P], F16)
        bias = sb("bias", [P, 2, M])
        gi_bias = sb("gi_bias", [P, M])
        bhn = sb("bhn", [P, K, B])
        wg_raw = sb("wg_raw", [P, K, E])
        wg = sb("wg", [P, K, P], F32R)
        mags = sb("mags", [P, 8])
        spare = sb("spare", [P, 1])
        sc = sb("sc", [P, 8])
        h_now = sb("h_now", [P, 2, K, B])
        h_parts = sb("h_parts", [P, K, 2, B], F16)
        h_log = sb("h_log", [P, K, TOK])
        rpre = sb("rpre", [P, 2, K, B])
        zpre = sb("zpre", [P, 2, K, B])
        rs = sb("rs", [P, K, B])
        zs = sb("zs", [P, K, B])
        hn1 = sb("hn1", [P, K, B])
        hn = sb("hn", [P, K, B])
        rh = sb("rh", [P, K, B])
        npre = sb("npre", [P, K, B])
        nt = sb("nt", [P, K, B])
        zh = sb("zh", [P, K, B])
        omz = sb("omz", [P, K, B])
        nmix = sb("nmix", [P, K, B])
        x_raw = sb("x_raw", [P, K, TOK])
        x_split = sb("x_split", [P, 2, K, TOK], F32R)
        wi_split = sb("wi_split", [P, 2, UCOLS], F32R)
        gi = sb("gi", [P, 2, M, TOK])
        assert M * TOK == K * M * P
        whh_raw = gi[:, 1].rearrange("p a b -> p (a b)").rearrange("p (k m) -> p k m", k=K)
        f_split = sb("f_split", [P, 2, K, TOK], F32R)
        w_raw = sb("w_raw", [P, 2, UCOLS])
        wu_split = sb("wu_split", [P, SPLITS, 2, UCOLS], F32R)
        sig = sb("sig", [P, TOK])
        hid = sb("hid", [P, TOK])
        hid_split = sb("hid_split", [P, 2, 2, TOK], F32R)
        scT = sb("scT", [2 * E, TOK])
        score = sb("score", [P, TT, E])
        score1 = sb("score1", [P, TT, E])
        top = sb("top", [P, TT, 8])
        top_i = sb("top_i", [P, TT, 8], U32)
        top_f = sb("top_f", [P, TT, 8])
        gap = sb("gap", [P, TT])
        prob = sb("prob", [P, 2, TT])
        w_1 = sb("w_1", [P, TT, E])
        w_2 = sb("w_2", [P, TT, E])
        w_te = sb("w_te", [P, TT, E])
        wT = sb("wT", [E, TOK])
        w_exp = sb("w_exp", [P, 2, TOK])
        y_sb = sb("y_sb", [P, TT, D])
        w_dram = nc.dram_tensor("w_scratch", [E, TOK], F32, kind="Internal").ap()

        y_ps = ps("y_ps", [P, TT, 512])
        a_ps = ps("a_ps", [P, 512])
        b_ps = ps("b_ps", [P, 512])
        gh_ps = ps("gh_ps", [P, M, 2, B])
        misc_ps = ps("misc_ps", [P, 512])

        GI_BANKS = (misc_ps, b_ps, misc_ps)

        whh_loaded = sem("whh_loaded")
        loaded = sem("loaded")
        const_ready = sem("const_ready")
        setup = sem("setup")
        mag_ready = sem("mag_ready")
        gh_ready = sem("gh_ready")
        gru_ops = sem("gru_ops")
        sig_rz = sem("sig_rz")
        tanh_n = sem("tanh_n")
        x_loaded = sem("x_loaded")
        x_hi = sem("x_hi")
        x_lo = sem("x_lo")
        wi_loaded = [sem("wi_loaded_0"), sem("wi_loaded_1")]
        wi_hi = sem("wi_hi")
        gi_mm = sem("gi_mm")
        gi_ready = sem("gi_ready")
        wu_loaded = [sem("wu_loaded_0"), sem("wu_loaded_1")]
        wu_hi = sem("wu_hi")
        split = sem("split")
        wu_used = sem("wu_used")
        a_mm = sem("a_mm")
        b_mm = sem("b_mm")
        sig_a = sem("sig_a")
        ffn_ops = sem("ffn_ops")
        hid_hi = sem("hid_hi")
        f_hi = sem("f_hi")
        f_lo = sem("f_lo")
        score_mm = sem("score_mm")
        route_ops = sem("route_ops")
        score_T = sem("score_T")
        probs = sem("probs")
        w_T = sem("w_T")
        wT_out = sem("wT_out")
        w_loaded = [sem("w_even_loaded"), sem("w_odd_loaded")]
        y_read = sem("y_read")
        xres_loaded = sem("xres_loaded")
        stored = sem("stored")

        SC_W, SC_H, SC_INV, SC_IH, SC_NH, SC_PW, SC_PH = range(7)

        def scale(i):
            return sc[:, i:i + 1]

        def walk(eng, prep, start, group, finish):
            prep(0, False)
            start(-1, True, False)
            with eng.Fori(0, GROUPS) as g:
                group(-1, g, False, True, False)
            prep(1, False)
            start(0, True, False)
            with eng.Fori(0, GROUPS) as g:
                group(0, g, True, True, False)
            prep(2, False)
            with eng.Fori(1, CHUNKS - 1) as c:
                start(c, True, True)
                with eng.Fori(0, GROUPS) as g:
                    group(c, g, True, True, True)
                prep(c + 2, True)
                finish(c)
            start(CHUNKS - 1, False, True)
            with eng.Fori(0, GROUPS) as g:
                group(CHUNKS - 1, g, True, False, True)
            finish(CHUNKS - 1)
            start(CHUNKS, False, True)
            with eng.Fori(0, GROUPS) as g:
                group(CHUNKS, g, False, False, True)
            finish(CHUNKS)

        def step_no(c, g, s):
            return c * STEPS + g * GS + s

        def unit_no(c, g, u):
            return (c - 1) * UNITS + g * UG + u

        def wi_no(c, p):
            return (c + 1) * WI + p

        def gate_no(c, p, j):
            return (c + 1) * M + p * MW + j

        WI_AT = 4

        def raw_of(u):
            return (u - 1) % 2 if 0 < u <= WI_AT else 1 if u == 0 else u % 2

        def loaded_before(c, g, u):
            same = [v for v in range(1, UG + 1) if raw_of(v) == raw_of(u)]
            return ((c - 1) * GROUPS + g) * len(same) + same.index(u) + 1 + raw_of(u)

        def pieces_before(c, g):
            if isinstance(c, int) and c < 1:
                return (c + 1) * WI + 2 + g
            steady = 2 * WI + 3
            if isinstance(c, int) and c >= CHUNKS - 1:
                return (steady + (CHUNKS - 2) * (WI + UNITS) - 1
                        + ((c - CHUNKS + 1) * GROUPS + g) * UG)
            return steady + (c - 1) * (WI + UNITS) + g * (1 + UG)

        CREDIT = 1

        def prev_in_ring(n, u):
            u %= UG
            return n - SPLITS if u >= SPLITS else n - u - (UG - u) % SPLITS - ((UG - u) % SPLITS == 0) * SPLITS

        N_ROUTE = 6 + 2 * TT + 3 * TT
        GAP = 5 + 2 * TT
        N_SMALL = 6 + K + E
        N_SETUP = N_SMALL + 14

        def settle(eng):
            if eng is nc.sync:
                eng.wait_ge(const_ready, 2)
            else:
                nc.vector.memset(spare[:], 0.0)

        block = ctx.enter_context(nc.Block())

        @block.sync
        def _(sp):
            sp.dma_start(h_now[:, 1], h0_feat).then_inc(loaded, 16)
            sp.dma_start(bias[:], b_feat).then_inc(loaded, 16)
            sp.dma_start(wg_raw[:], w_gate).then_inc(loaded, 16)

            def prep(n, ffn):
                settle(nc.sync)
                sp.wait_ge(x_lo, n + CREDIT)
                sp.dma_start(x_raw[:], x_feat[bass.ds(n % CHUNKS, 1)].rearrange("o p k t -> (o p) k t")
                             ).then_inc(x_loaded, 16)
                if isinstance(n, int) and n == 2:
                    sp.wait_ge(split, pieces_before(0, 0) + CREDIT)
                    sp.dma_start(w_raw[:, 1], w_units[0]).then_inc(wu_loaded[1], 16)
                load_wi(0, 0, pieces_before(n - 2, GROUPS - 1) + UG if ffn else WI * n)

            def load_wi(row, slot, pieces):
                settle(nc.sync)
                sp.wait_ge(split, pieces + CREDIT)
                sp.dma_start(w_raw[:, slot], w_inproj[bass.ds(row, 1)].rearrange("o p n -> (o p) n")
                             ).then_inc(wi_loaded[slot], 16)

            def start(c, proj, ffn):
                if proj:
                    load_wi(1, 1, pieces_before(c, 0) - 2 if ffn else WI * (c + 1))

            def group(c, g, rec, proj, ffn):
                if proj and not ffn:
                    load_wi(2 + g, 0, pieces_before(c, g) + g - 1)
                for u in range(1, UG + 1) if ffn else []:
                    before = pieces_before(c, g)
                    if proj and u == WI_AT + 1:
                        load_wi(2 + g, 0, before + WI_AT - 1)
                    if proj:
                        last = u - 2 + (u > WI_AT)
                    elif u <= WI_AT:
                        last = u - 2 + (u == 1 and isinstance(c, int) and c == CHUNKS - 1)
                    else:
                        last = {WI_AT + 1: WI_AT, WI_AT + 2: WI_AT - 1}.get(u, u - 2)
                    settle(nc.sync)
                    sp.wait_ge(split, before + last + CREDIT)
                    row = g * UG + u if u < UG else g * -UG + UG
                    sp.dma_start(w_raw[:, raw_of(u)], w_units[bass.ds(row, 1)].rearrange("o p n -> (o p) n")
                                 ).then_inc(wu_loaded[raw_of(u)], 16)

            walk(sp, prep, start, group, lambda c: None)

        @block.gpsimd
        def _(pool):
            nc.gpsimd.memset(ident[:], 0.0).then_inc(const_ready, 1)
            pool.wait_ge(const_ready, 1)
            nc.gpsimd.affine_select(out=ident[:], in_=ident[:], compare_op=ALU.not_equal, fill=1.0,
                                    base=0, pattern=[[-1, P]], channel_multiplier=1
                                    ).then_inc(const_ready, 1)
            pool.wait_ge(const_ready, 2)
            pool.wait_ge(setup, N_SMALL + 3)
            nc.gpsimd.partition_all_reduce(mags[:, 4:5], mags[:, 2:3], P, RMAX).then_inc(mag_ready, 1)
            nc.gpsimd.partition_all_reduce(mags[:, 5:6], mags[:, 3:4], P, RMAX).then_inc(mag_ready, 1)

            for f in range(CHUNKS):
                if f:
                    pool.wait_ge(stored, 16 * f)
                pool.dma_start(y_sb[:], x_tok[bass.ds(f * TOK, TOK), :].rearrange(
                    "(t p) d -> p t d", p=P)).then_inc(xres_loaded, 16)
                pool.wait_ge(route_ops, N_ROUTE * (f + 1))
                if f:
                    for e in range(2):
                        pool.wait_ge(w_loaded[e], 16 * (E // 2) * f)
                pool.dma_start(w_dram, wT[:]).then_inc(wT_out, 16)
                pool.wait_ge(wT_out, 16 * (f + 1))
                for e in range(E):
                    last = UNITS * f - 1 if e < 2 else UNITS * f + ((e - 1) * HE - 1) // P
                    pool.wait_ge(ffn_ops, FFN_OPS * (last + 1) + WEIGHTED)
                    pool.dma_start(w_exp[:, e % 2], w_dram[e:e + 1, :].to_broadcast([P, TOK])
                                   ).then_inc(w_loaded[e % 2], 16)
                pool.wait_ge(y_read, TT * (f + 1) + CREDIT)
                pool.dma_start(out[bass.ds(f * TOK, TOK), :].rearrange("(t p) d -> p t d", p=P),
                               y_sb[:]).then_inc(stored, 16)
            pool.wait_ge(stored, 16 * CHUNKS)

        @block.scalar
        def _(act):
            def prep(n, ffn):
                act.wait_ge(x_loaded, 16 * (n + 1))
                act.wait_ge(gi_mm, M * n + CREDIT)
                nc.scalar.copy(x_split[:, 0], x_raw[:]).then_inc(x_hi, 1)
                if isinstance(n, int) and n == 2:
                    split_wu(1, 0, 0)
                split_wi(n - 1, 0, 0)
                if isinstance(n, int) and n == 1:
                    act.wait_ge(setup, N_SETUP)

            def split_wi(c, p, slot):
                there = c + 2 if slot else (c + 1) * (WI - 1) + (p - 1 if not isinstance(p, int) or p else 0) + 1
                act.wait_ge(wi_loaded[slot], 16 * there)
                act.wait_ge(gi_mm, gate_no(c, p, 0) + CREDIT)
                nc.scalar.copy(wi_split[:, 0], w_raw[:, slot]).then_inc(wi_hi, 1)

            def split_wu(c, g, u):
                n = unit_no(c, g, u)
                act.wait_ge(wu_loaded[raw_of(u)], 16 * (loaded_before(c, g, u) if u else 1))
                act.wait_ge(wu_used, prev_in_ring(n, u) + 1 + SPLITS)
                nc.scalar.copy(wu_split[:, u % UG % SPLITS, 0], w_raw[:, raw_of(u)]).then_inc(wu_hi, 1)

            def take_gi(c, p, j, src):
                act.wait_ge(gi_mm, gate_no(c, p, j) + 1 + CREDIT)
                m = p * MW + j
                nc.scalar.activation(gi[:, bass.ds((c + 1) % 2, 1), bass.ds(m, 1), :], src[:], ACT.Identity,
                                     bias=gi_bias[:, bass.ds(m, 1)]).then_inc(gi_ready, 1)

            def start(c, proj, ffn):
                if ffn:
                    f = c - 1
                    act.wait_ge(gru_ops, GRU_OPS * STEPS * c + CREDIT)
                    act.wait_ge(b_mm, UNITS * f + CREDIT)
                    nc.scalar.copy(f_split[:, 0], h_log[:]).then_inc(f_hi, 1)
                if proj:
                    for j in range(MW):
                        take_gi(c, 0, j, GI_BANKS[j])
                    split_wi(c, 1, 1)
                if ffn:
                    act.wait_ge(route_ops, N_ROUTE * f + GAP)
                    nc.scalar.activation(prob[:, 0], gap[:], ACT.Sigmoid).then_inc(probs, 1)
                    nc.scalar.activation(prob[:, 1], gap[:], ACT.Sigmoid, scale=-1.0).then_inc(probs, 1)
                if proj:
                    for j in range(MW):
                        take_gi(c, 1, j, GI_BANKS[j])

            def group(c, g, rec, proj, ffn):
                if proj and not ffn:
                    split_wi(c, 2 + g, 0)
                for s in range(GS):
                    if rec:
                        t = step_no(c, g, s)
                        act.wait_ge(gru_ops, GRU_OPS * t + R_B + CREDIT)
                        nc.scalar.activation(rs[:], rpre[:, 1], ACT.Sigmoid).then_inc(sig_rz, 1)
                        act.wait_ge(gru_ops, GRU_OPS * t + Z_B + CREDIT)
                        nc.scalar.activation(zs[:], zpre[:, 1], ACT.Sigmoid).then_inc(sig_rz, 1)
                        act.wait_ge(gru_ops, GRU_OPS * t + N_PRE + CREDIT)
                        nc.scalar.activation(nt[:], npre[:], ACT.Tanh).then_inc(tanh_n, 1)
                    for kind, i in BLOCKS[s]:
                        if kind == "G" and i == MW - 1 and ffn:
                            split_wu(c, g, UG)
                        if kind == "G" and proj:
                            take_gi(c, 2 + g, i, misc_ps)
                        if kind == "A" and ffn:
                            n = unit_no(c, g, i)
                            if i + 1 < UG:
                                split_wu(c, g, i + 1)
                            act.wait_ge(a_mm, n + 1)
                            nc.scalar.activation(sig[:], a_ps[:], ACT.Sigmoid, scale=scale(SC_IH)
                                                 ).then_inc(sig_a, 1)
                        if kind == "B" and ffn:
                            n = unit_no(c, g, i)
                            act.wait_ge(ffn_ops, FFN_OPS * (n + 1) + WEIGHTED)
                            act.wait_ge(wu_used, n + SPLITS - (1 if i else 0))
                            nc.scalar.copy(hid_split[:, i % 2, 0], hid[:]).then_inc(hid_hi, 1)
                            if i == WI_AT - 1 and proj:
                                split_wi(c, 2 + g, 0)

            act.sem_inc(gi_ready, CREDIT)
            act.wait_ge(setup, N_SMALL)
            act.wait_ge(x_loaded, 16)
            act.dma_start(whh_raw[:], w_hh).then_inc(whh_loaded, 16)
            walk(act, prep, start, group, lambda c: None)

        @block.vector
        def _(dve):
            done = [0]

            def chain(ins):
                done[0] += 1
                ins.then_inc(setup, 1)
                dve.wait_ge(setup, done[0])

            V = nc.vector
            dve.sem_inc(ffn_ops, FFN_OPS)
            for credited in (x_lo, split, gru_ops, y_read):
                dve.sem_inc(credited, CREDIT)
            dve.wait_ge(loaded, 48)
            chain(V.tensor_copy(gi_bias[:], bias[:, 0]))
            chain(V.tensor_tensor(gi_bias[:, 0:2 * K], bias[:, 0, 0:2 * K], bias[:, 1, 0:2 * K], ALU.add))
            chain(V.tensor_copy(bhn[:], bias[:, 1, 2 * K:M].unsqueeze(2).to_broadcast([P, K, B])))
            chain(V.memset(zeros_r[:].bitcast(F32), 0.0))
            for k in range(K):
                chain(V.tensor_copy(wg[:, k], zeros_r[:].bitcast(F32)))
            chain(V.tensor_copy(wg[:, :, 0:E], wg_raw[:]))
            chain(V.tensor_tensor(wg[:, :, E:2 * E], wg_raw[:], wg[:, :, 0:E].bitcast(F32), ALU.subtract))
            for e in range(E):
                chain(V.memset(iota_e[:, e:e + 1], float(e)))
            assert done[0] == N_SMALL, done[0]

            def scales():
                dve.wait_ge(whh_loaded, 16)
                chain(V.tensor_reduce(mags[:, 2:3], whh_raw[:], AX_XY, ALU.max, apply_absolute_value=True))
                chain(V.tensor_reduce(mags[:, 3:4], h_now[:, 1], AX_XY, ALU.max, apply_absolute_value=True))
                chain(V.tensor_scalar(mags[:, 3:4], mags[:, 3:4], 1.0, None, ALU.max))
                dve.wait_ge(mag_ready, 2)
                chain(V.tensor_scalar(mags[:, 4:6], mags[:, 4:6], 2.0 ** -40, None, ALU.max))
                chain(V.tensor_scalar(sc[:, SC_PW:SC_PH + 1].bitcast(I32), mags[:, 4:6].bitcast(I32),
                                      0x7F800000, None, ALU.bitwise_and))
                chain(V.tensor_scalar(sc[:, SC_W:SC_H + 1].bitcast(I32), sc[:, SC_PW:SC_PH + 1].bitcast(I32),
                                      -1.0, float((127 + 14 + 127) << 23), ALU.mult, ALU.add))
                chain(V.tensor_scalar(sc[:, SC_IH:SC_IH + 1], scale(SC_PH), 2.0 ** -14, None, ALU.mult))
                chain(V.tensor_scalar(sc[:, SC_INV:SC_INV + 1], scale(SC_PW), 2.0 ** -14, scale(SC_IH),
                                      ALU.mult, ALU.mult))
                chain(V.tensor_scalar(sc[:, SC_NH:SC_NH + 1], scale(SC_H), -1.0, None, ALU.mult))

            def recurrent_weights():
                chain(V.tensor_scalar(whh[:, 0], whh_raw[:], scale(SC_W), None, ALU.mult))
                chain(V.scalar_tensor_tensor(out=whh[:, 1], in0=whh_raw[:], scalar=scale(SC_W),
                                             in1=whh[:, 0], op0=ALU.mult, op1=ALU.subtract))
                chain(V.tensor_scalar(h_now[:, 0], h_now[:, 1], scale(SC_H), None, ALU.mult))
                chain(V.tensor_copy(h_parts[:, :, 0], h_now[:, 0]))
                chain(V.tensor_tensor(h_parts[:, :, 1], h_now[:, 0], h_parts[:, :, 0], ALU.subtract))
                assert done[0] == N_SETUP, done[0]

            def prep(n, ffn):
                dve.wait_ge(x_hi, n + 1)
                V.tensor_tensor(x_split[:, 1], x_raw[:], x_split[:, 0].bitcast(F32), ALU.subtract
                                ).then_inc(x_lo, 1)
                if isinstance(n, int) and n == 2:
                    split_wu(1, 0, 0)
                split_wi(n - 1, 0, 0)
                if isinstance(n, int) and n == 1:
                    recurrent_weights()

            def split_wi(c, p, slot):
                dve.wait_ge(wi_hi, wi_no(c, p) + 1)
                V.tensor_tensor(wi_split[:, 1], w_raw[:, slot], wi_split[:, 0].bitcast(F32), ALU.subtract
                                ).then_inc(split, 1)

            def split_wu(c, g, u):
                dve.wait_ge(wu_hi, unit_no(c, g, u) + 1)
                b = u % UG % SPLITS
                V.tensor_tensor(wu_split[:, b, 1], w_raw[:, raw_of(u)],
                                wu_split[:, b, 0].bitcast(F32), ALU.subtract
                                ).then_inc(split, 1)

            def route(c, proj):
                f = c - 1
                base = N_ROUTE * f
                n = [0]

                def op(ins, wait=True):
                    ins.then_inc(route_ops, 1)
                    n[0] += 1
                    if wait:
                        dve.wait_ge(route_ops, base + n[0])

                dve.wait_ge(score_mm, f + 1)
                op(V.tensor_copy(scT[:], a_ps[0:2 * E, :]), False)
                if proj:
                    split_wi(c, 1, 1)
                dve.wait_ge(score_T, f + 1)
                halves = b_ps[:, 0:TT * 2 * E].rearrange("p (t e) -> p t e", t=TT)
                op(V.tensor_scalar(score1[:], halves[:, :, 0:E], scale(SC_IH), None, ALU.mult))
                op(V.scalar_tensor_tensor(out=score[:], in0=halves[:, :, E:2 * E], scalar=scale(SC_IH),
                                          in1=score1[:], op0=ALU.mult, op1=ALU.add))
                settle(nc.vector)
                for t in range(TT):
                    op(V.max(top[:, t], score[:, t]), t == TT - 1)
                settle(nc.vector)
                for t in range(TT):
                    op(V.max_index(top_i[:, t], top[:, t], score[:, t]), t == TT - 1)
                op(V.tensor_copy(top_f[:], top_i[:]))
                op(V.tensor_tensor(gap[:], top[:, :, 0], top[:, :, 1], ALU.subtract))
                assert n[0] == GAP
                dve.wait_ge(probs, 2 * (f + 1))
                for t in range(TT):
                    op(V.tensor_scalar(w_1[:, t], iota_e[:], top_f[:, t, 0:1], prob[:, 0, t:t + 1],
                                       ALU.is_equal, ALU.mult), False)
                for t in range(TT):
                    op(V.tensor_scalar(w_2[:, t], iota_e[:], top_f[:, t, 1:2], prob[:, 1, t:t + 1],
                                       ALU.is_equal, ALU.mult), t == TT - 1)
                for t in range(TT):
                    op(V.tensor_tensor(w_te[:, t], w_1[:, t], w_2[:, t], ALU.add), False)
                dve.wait_ge(w_T, f + 1)
                dve.wait_ge(xres_loaded, 16 * c)
                op(V.tensor_copy(wT[:], a_ps[0:E, :]), False)
                assert n[0] == N_ROUTE, n[0]

            def start(c, proj, ffn):
                if ffn:
                    dve.wait_ge(f_hi, c)
                    V.tensor_tensor(f_split[:, 1], h_log[:], f_split[:, 0].bitcast(F32), ALU.subtract
                                    ).then_inc(f_lo, 1)
                    route(c, proj)
                elif proj:
                    split_wi(c, 1, 1)
                    if c == -1:
                        scales()

            def gru_step(c, g, s):
                t = step_no(c, g, s)
                now, new = s % 2, (s + 1) % 2
                at = g * (GS * B) + s * B
                gi_c = gi[:, bass.ds(c % 2, 1), :, bass.ds(at, B)].rearrange("p o m b -> p (o m) b")
                inv = scale(SC_INV)

                def after(k):
                    dve.wait_ge(gru_ops, GRU_OPS * t + k + CREDIT)

                def op(ins):
                    ins.then_inc(gru_ops, 1)

                if s == 0:
                    dve.wait_ge(gi_ready, M * (c + 1) + CREDIT)
                dve.wait_ge(gh_ready, t + 1)
                op(V.scalar_tensor_tensor(out=rpre[:, 0], in0=gh_ps[:, 0:K, 0, :], scalar=inv,
                                          in1=gi_c[:, 0:K], op0=ALU.mult, op1=ALU.add))
                op(V.scalar_tensor_tensor(out=hn1[:], in0=gh_ps[:, 2 * K:M, 0, :], scalar=inv,
                                          in1=bhn[:], op0=ALU.mult, op1=ALU.add))
                after(R_A)
                op(V.scalar_tensor_tensor(out=rpre[:, 1], in0=gh_ps[:, 0:K, 1, :], scalar=inv,
                                          in1=rpre[:, 0], op0=ALU.mult, op1=ALU.add))
                after(HN_A)
                op(V.scalar_tensor_tensor(out=hn[:], in0=gh_ps[:, 2 * K:M, 1, :], scalar=inv,
                                          in1=hn1[:], op0=ALU.mult, op1=ALU.add))
                op(V.scalar_tensor_tensor(out=zpre[:, 0], in0=gh_ps[:, K:2 * K, 0, :], scalar=inv,
                                          in1=gi_c[:, K:2 * K], op0=ALU.mult, op1=ALU.add))
                after(HN_B)
                dve.wait_ge(sig_rz, 2 * t + 1)
                op(V.tensor_tensor(rh[:], rs[:], hn[:], ALU.mult))
                after(Z_A)
                op(V.scalar_tensor_tensor(out=zpre[:, 1], in0=gh_ps[:, K:2 * K, 1, :], scalar=inv,
                                          in1=zpre[:, 0], op0=ALU.mult, op1=ALU.add))
                after(R_HN)
                op(V.tensor_tensor(npre[:], rh[:], gi_c[:, 2 * K:M], ALU.add))
                dve.wait_ge(sig_rz, 2 * t + 2)
                op(V.tensor_tensor(zh[:], zs[:], h_now[:, now], ALU.mult))
                op(V.tensor_scalar(omz[:], zs[:], scale(SC_NH), scale(SC_H), ALU.mult, ALU.add))
                after(ONE_Z)
                dve.wait_ge(tanh_n, t + 1)
                op(V.tensor_tensor(nmix[:], nt[:], omz[:], ALU.mult))
                after(N_MIX)
                op(V.tensor_tensor(h_parts[:, :, 0], nmix[:], zh[:], ALU.add))
                op(V.tensor_tensor(h_now[:, new], nmix[:], zh[:], ALU.add))
                after(H_NEW)
                op(V.tensor_tensor(h_parts[:, :, 1], h_now[:, new], h_parts[:, :, 0], ALU.subtract))
                op(V.tensor_copy(h_log[:, :, bass.ds(at, B)], h_now[:, new]))

            def group(c, g, rec, proj, ffn):
                if proj and not ffn:
                    split_wi(c, 2 + g, 0)
                for s in range(GS):
                    if rec:
                        gru_step(c, g, s)
                    for kind, i in BLOCKS[s] if ffn else []:
                        if kind == "G" and i == MW - 1:
                            split_wu(c, g, UG)
                        n = unit_no(c, g, i)
                        at = FFN_OPS * (n + 1)
                        if kind == "A":
                            early = ("Y", i - 2) not in BLOCKS[s]
                            if i + 1 < UG and early:
                                split_wu(c, g, i + 1)
                            dve.wait_ge(sig_a, n + 1)
                            dve.wait_ge(ffn_ops, at)
                            V.scalar_tensor_tensor(out=hid[:], in0=a_ps[:], scalar=scale(SC_IH),
                                                   in1=sig[:], op0=ALU.mult, op1=ALU.mult
                                                   ).then_inc(ffn_ops, 1)
                            if i + 1 < UG and not early:
                                split_wu(c, g, i + 1)
                        if kind == "B":
                            dve.wait_ge(b_mm, n + 1 + CREDIT)
                            dve.wait_ge(ffn_ops, at + SILU)
                            V.scalar_tensor_tensor(out=hid[:], in0=b_ps[:], scalar=scale(SC_IH),
                                                   in1=hid[:], op0=ALU.mult, op1=ALU.mult
                                                   ).then_inc(ffn_ops, 1)
                            for e, r0, r1 in experts_of(i):
                                if e * HE >= i * P:
                                    dve.wait_ge(w_loaded[e % 2], 16 * ((c - 1) * (E // 2) + g * (EG // 2) + e // 2 + 1))
                                if r0 == 0:
                                    dve.wait_ge(ffn_ops, at + GATED)
                                ins = V.tensor_tensor(hid[r0:r1], hid[r0:r1], w_exp[r0:r1, e % 2], ALU.mult)
                            ins.then_inc(ffn_ops, 1)
                            dve.wait_ge(hid_hi, n + 1)
                            V.tensor_tensor(hid_split[:, i % 2, 1], hid[:],
                                            hid_split[:, i % 2, 0].bitcast(F32), ALU.subtract
                                            ).then_inc(ffn_ops, 1)
                            if i == WI_AT - 1 and proj:
                                split_wi(c, 2 + g, 0)

            def finish(c):
                f = c - 1
                dve.wait_ge(wu_used, SPLITS + UNITS * (f + 1))
                dve.wait_ge(xres_loaded, 16 * (f + 1))
                for t in range(TT):
                    V.tensor_tensor(y_sb[:, t], y_ps[:, t], y_sb[:, t], ALU.add).then_inc(y_read, 1)

            walk(dve, prep, start, group, finish)

        @block.tensor
        def _(pe):
            PARTS = ((0, 0), (0, 1), (1, 0))
            pe.sem_inc(wu_used, SPLITS)
            for credited in (gi_mm, b_mm):
                pe.sem_inc(credited, CREDIT)

            def recur(c, g, s):
                t = step_no(c, g, s)
                pe.wait_ge(gru_ops, GRU_OPS * t + CREDIT)
                for m in range(M):
                    for k in range(K):
                        for part in range(2):
                            mm = pe.matmul(gh_ps[:, m].rearrange("p a b -> p (a b)"),
                                           whh[:, part, k, m * P:(m + 1) * P],
                                           h_parts[:, k].rearrange("p a b -> p (a b)"),
                                           start=(k == 0 and part == 0), stop=(k == K - 1 and part == 1))
                mm.then_inc(gh_ready, 1)

            def project(c, p, j, dst, before):
                if j == 0:
                    pe.wait_ge(x_lo, c + 2 + CREDIT)
                    third = 1 if isinstance(c, int) and c < 1 else WI_AT + 1
                    at = pieces_before(c, 0) + p - 1 if isinstance(p, int) and p < 2 else pieces_before(c, p - 2) + third
                    pe.wait_ge(split, at + CREDIT)
                pe.wait_ge(gi_ready, gate_no(c, p, j) + 1 - before + CREDIT)
                for i, (a, b) in enumerate(PARTS):
                    for k in range(K):
                        mm = pe.matmul(dst[:], wi_split[:, a, (j * K + k) * P:(j * K + k + 1) * P],
                                       x_split[:, b, k], start=(i == 0 and k == 0),
                                       stop=(i == 2 and k == K - 1))
                mm.then_inc(gi_mm, 1)

            def up(c, g, u, dst, col, signal, proj):
                n = unit_no(c, g, u)
                if signal is a_mm:
                    if u == 0:
                        pe.wait_ge(route_ops, N_ROUTE * c)
                    pe.wait_ge(split, pieces_before(c, g) + u + (proj and u > WI_AT) + CREDIT)
                    pe.wait_ge(ffn_ops, FFN_OPS * n + SILU)
                else:
                    if u == 0 and proj:
                        pe.wait_ge(gi_ready, gate_no(c, 1, 2) + CREDIT)
                    pe.wait_ge(ffn_ops, FFN_OPS * n + GATED)
                for i, (a, b) in enumerate(PARTS):
                    for k in range(K):
                        mm = pe.matmul(dst[:], wu_split[:, u % SPLITS, a, col + k * P:col + (k + 1) * P],
                                       f_split[:, b, k], start=(i == 0 and k == 0),
                                       stop=(i == 2 and k == K - 1))
                mm.then_inc(signal, 1)

            def down(c, g, u):
                n = unit_no(c, g, u)
                pe.wait_ge(ffn_ops, FFN_OPS * (n + 1) + HID_LO)
                for t in range(TT):
                    for a, b in PARTS:
                        mm = pe.matmul(y_ps[:, t], hid_split[:, u % 2, a, t * P:(t + 1) * P],
                                       wu_split[:, u % SPLITS, b, W3:W3 + D],
                                       start=False, stop=True, skip_group_check=True)
                mm.then_inc(wu_used, 1)

            def scores(f):
                pe.wait_ge(f_lo, f + 1)
                pe.wait_ge(ffn_ops, FFN_OPS * (UNITS * f + 1))
                for b in range(2):
                    for k in range(K):
                        mm = pe.matmul(a_ps[:], wg[:, k], f_split[:, b, k],
                                       start=(b == 0 and k == 0), stop=(b == 1 and k == K - 1))
                mm.then_inc(score_mm, 1)
                pe.wait_ge(route_ops, N_ROUTE * f + 1)
                for t in range(TT):
                    mm = pe.matmul(b_ps[:, t * 2 * E:(t + 1) * 2 * E], scT[:, t * P:(t + 1) * P],
                                   ident[0:2 * E, 0:2 * E])
                mm.then_inc(score_T, 1)

            def clear_y(f):
                pe.wait_ge(y_read, TT * f + CREDIT)
                for t in range(TT):
                    pe.matmul(y_ps[:, t], zeros_r[:], wg[:].rearrange("p k n -> p (k n)"), start=True, stop=True,
                              skip_group_check=True)

            def weights_T(f):
                pe.wait_ge(route_ops, N_ROUTE * (f + 1) - 1)
                for t in range(TT):
                    mm = pe.matmul(a_ps[0:E, t * P:(t + 1) * P], w_te[:, t], ident[:])
                mm.then_inc(w_T, 1)

            def start(c, proj, ffn):
                if proj:
                    project(c, 0, 0, GI_BANKS[0], 1)
                    if ffn:
                        pe.wait_ge(ffn_ops, FFN_OPS * (UNITS * (c - 1) + 1))
                    project(c, 0, 1, GI_BANKS[1], 2)
                    project(c, 0, 2, GI_BANKS[2], 2)
                if ffn:
                    if proj:
                        pe.wait_ge(gi_ready, gate_no(c, 0, 2) + CREDIT)
                    scores(c - 1)
                    clear_y(c - 1)
                if proj:
                    project(c, 1, 0, GI_BANKS[0], 1)
                    if ffn:
                        pe.wait_ge(route_ops, N_ROUTE * (c - 1) + 4)
                    project(c, 1, 1, GI_BANKS[1], 2)
                if ffn:
                    weights_T(c - 1)
                if proj:
                    project(c, 1, 2, GI_BANKS[2], 2)

            def group(c, g, rec, proj, ffn):
                for s in range(GS):
                    if rec:
                        recur(c, g, s)
                    for kind, i in BLOCKS[s]:
                        if kind == "G" and proj:
                            project(c, 2 + g, i, misc_ps, 1)
                        elif kind == "A" and ffn:
                            up(c, g, i, a_ps, W1, a_mm, proj)
                        elif kind == "B" and ffn:
                            up(c, g, i, b_ps, W2, b_mm, proj)
                        elif kind == "Y" and ffn:
                            down(c, g, i)

            def prep(n, ffn):
                if isinstance(n, int) and n == 1:
                    pe.wait_ge(setup, N_SETUP)
                    pe.wait_ge(const_ready, 2)

            walk(pe, prep, start, group, lambda c: None)

def kernel(x, cond_2048, L0_cond_W_ih, L0_cond_W_hh, L0_cond_b_ih, L0_cond_b_hh,
           L0_ffn_Wg, L0_ffn_W1, L0_ffn_W2, L0_ffn_W3):
    import numpy as np
    import concourse.bacc as bacc
    from concourse import mybir as mb
    from concourse.bass_utils import run_bass_kernel_spmd

    x = np.asarray(x)
    B, T, D = x.shape
    K, M = D // P, 3 * D // P
    E, H, _ = np.asarray(L0_ffn_W1).shape
    STEPS, WI = 32, 4
    CHUNKS, TOK = T // STEPS, STEPS * B

    x_tok = np.ascontiguousarray(x.transpose(1, 0, 2)).reshape(T * B, D)
    x_feat = np.ascontiguousarray(x_tok.reshape(CHUNKS, TOK, K, P).transpose(0, 3, 2, 1))

    def feat(w):
        return np.ascontiguousarray(w.reshape(K, P, -1).transpose(1, 0, 2))

    w1, w2 = np.asarray(L0_ffn_W1).reshape(E * H, D), np.asarray(L0_ffn_W2).reshape(E * H, D)
    w3 = np.asarray(L0_ffn_W3).transpose(0, 2, 1).reshape(-1, P, D)

    def up_unit(w):
        return w.reshape(-1, P, K, P).transpose(0, 3, 2, 1).reshape(-1, P, K * P)

    w_units = np.ascontiguousarray(np.concatenate([up_unit(w1), up_unit(w2), w3], axis=2))
    w_ih = np.asarray(L0_cond_W_ih)
    w_inproj = np.ascontiguousarray(
        w_ih.reshape(K, P, WI, M // WI, P).transpose(2, 1, 3, 0, 4)).reshape(WI, P, -1)
    b_feat = np.ascontiguousarray(
        np.stack([np.asarray(L0_cond_b_ih), np.asarray(L0_cond_b_hh)]).reshape(2, M, P).transpose(2, 0, 1))

    arrays = {
        "x_feat": x_feat,
        "x_tok": x_tok,
        "h0_feat": feat(np.asarray(cond_2048).T),
        "w_hh": feat(np.asarray(L0_cond_W_hh)),
        "b_feat": b_feat,
        "w_gate": feat(np.asarray(L0_ffn_Wg).T),
        "w_units": w_units,
        "w_inproj": w_inproj,
    }
    nc = bacc.Bacc("TRN2", target_bir_lowering=False, num_devices=1, dynamic_dma_scratch_size=4096)
    args = [nc.dram_tensor(f"in_{n}", a.shape, mb.dt.from_np(a.dtype), kind="ExternalInput").ap()
            for n, a in arrays.items()]
    y = nc.dram_tensor("out_y", (T * B, D), mb.dt.float32, kind="ExternalOutput").ap()
    gru_moe_kernel(nc, *args, y)
    r = run_bass_kernel_spmd(nc, [{f"in_{n}": a for n, a in arrays.items()}], core_ids=[0])
    return np.ascontiguousarray(r.results[0]["out_y"].reshape(T, B, D).transpose(1, 0, 2))
```

```python
from contextlib import ExitStack

import concourse.bass as bass
from concourse import mybir

F32 = mybir.dt.float32
F32R = mybir.dt.float32r
F16 = mybir.dt.float16
I32 = mybir.dt.int32
U32 = mybir.dt.uint32
ALU = mybir.AluOpType
ACT = mybir.ActivationFunctionType
AX_X = mybir.AxisListType.X
AX_XY = mybir.AxisListType.XY
RMAX = bass.bass_isa.ReduceOp.max

P = 128


def gru_moe_kernel(nc, x_feat, x_tok, h0_feat, w_hh, b_feat, w_gate, w_units, w_inproj, out):
    CHUNKS, _, K, TOK = x_feat.shape
    B = h0_feat.shape[2]
    D = K * P
    M = 3 * K
    E = w_gate.shape[2]
    UNITS = w_units.shape[0]
    GROUPS = 2
    STEPS = TOK // B
    GS = STEPS // GROUPS
    UG = UNITS // GROUPS
    EG = E // GROUPS
    HE = UNITS * P // E
    WI = w_inproj.shape[0]
    MW = M // WI
    assert WI == 2 + GROUPS and UG * P == EG * HE
    TT = TOK // P
    W1, W2, W3 = 0, K * P, 2 * K * P
    UCOLS = 3 * K * P
    SPLITS = 3
    assert MW * K * P == UCOLS and UG % 2 == 1 and EG % 2 == 0

    def blocks(proj, last):
        gates = {4: 0, 6: 1, 8: 2} if last else {4: 0, 7: 1}
        order = []
        for u in range(UG):
            order += [("A", u), ("B", u)] + [("Y", u - 1)] * (u > 0)
            order += [("G", gates.get(u))] * (proj and u in gates)
        order += [("G", MW - 1)] * (proj and not last) + [("Y", UG - 1)]
        cuts = [(len(order) * s + GS // 2) // GS for s in range(GS + 1)]
        return [order[a:b] for a, b in zip(cuts, cuts[1:])]

    def experts_of(u):
        rows = []
        for e in range(u * P // HE, ((u + 1) * P - 1) // HE + 1):
            r0, r1 = max(0, e * HE - u * P), min(P, (e + 1) * HE - u * P)
            if r0 == 32 and r1 > 64:
                rows.append((e, r0, 64))
                r0 = 64
            rows.append((e, r0, r1))
        return rows

    BESIDE = "R_A HN_A R_B HN_B Z_A R_HN Z_B N_PRE Z_H ONE_Z N_MIX H_HI H_NEW H_LO".split()
    ALONE = "R_A R_B HN_A HN_B R_HN N_PRE Z_A Z_B N_H Z_NH H_HI H_NEW H_LO".split()
    GRU_OPS = len(BESIDE)
    (SILU, GATED, WEIGHTED, HID_LO) = range(1, 5)
    FFN_OPS = 4

    with ExitStack() as ctx:
        def sb(name, shape, dt=F32):
            return ctx.enter_context(nc.sbuf_tensor(name, shape, dt))

        def ps(name, shape):
            return ctx.enter_context(nc.psum_tensor(name, shape, F32))

        def sem(name):
            return ctx.enter_context(nc.semaphore(name))

        ident = sb("ident", [P, P])
        iota_e = sb("iota_e", [P, E])
        zeros_r = sb("zeros_r", [P, P], F32R)
        whh = sb("whh", [P, 2, K, M * P], F16)
        bias = sb("bias", [P, 2, M])
        gi_bias = sb("gi_bias", [P, M])
        bhn = sb("bhn", [P, K, B])
        wg_raw = sb("wg_raw", [P, K, E])
        wg = sb("wg", [P, K, P], F32R)
        mags = sb("mags", [P, 8])
        spare = sb("spare", [P, 1])
        sc = sb("sc", [P, 8])
        h_now = sb("h_now", [P, 2, K, B])
        h_parts = sb("h_parts", [P, K, 2, B], F16)
        h_log = sb("h_log", [P, K, TOK])
        rpre = sb("rpre", [P, 2, K, B])
        zpre = sb("zpre", [P, 2, K, B])
        rs = sb("rs", [P, K, B])
        zs = sb("zs", [P, K, B])
        hn1 = sb("hn1", [P, K, B])
        hn = sb("hn", [P, K, B])
        rh = sb("rh", [P, K, B])
        npre = sb("npre", [P, K, B])
        nt = sb("nt", [P, K, B])
        zh = sb("zh", [P, K, B])
        omz = sb("omz", [P, K, B])
        nmix = sb("nmix", [P, K, B])
        nmh = sb("nmh", [P, K, B])
        znh = sb("znh", [P, K, B])
        x_raw = sb("x_raw", [P, K, TOK])
        x_split = sb("x_split", [P, 2, K, TOK], F32R)
        wi_split = sb("wi_split", [P, 2, UCOLS], F32R)
        gi = sb("gi", [P, 2, M, TOK])
        assert M * TOK == K * M * P
        whh_raw = gi[:, 1].rearrange("p a b -> p (a b)").rearrange("p (k m) -> p k m", k=K)
        f_split = sb("f_split", [P, 2, K, TOK], F32R)
        w_raw = sb("w_raw", [P, 2, UCOLS])
        wu_split = sb("wu_split", [P, SPLITS, 2, UCOLS], F32R)
        sig = sb("sig", [P, TOK])
        hid = sb("hid", [P, TOK])
        hid_split = sb("hid_split", [P, 2, 2, TOK], F32R)
        scT = sb("scT", [2 * E, TOK])
        score = sb("score", [P, TT, E])
        score1 = sb("score1", [P, TT, E])
        top = sb("top", [P, TT, 8])
        top_i = sb("top_i", [P, TT, 8], U32)
        top_f = sb("top_f", [P, TT, 8])
        gap = sb("gap", [P, TT])
        prob = sb("prob", [P, 2, TT])
        w_1 = sb("w_1", [P, TT, E])
        w_2 = sb("w_2", [P, TT, E])
        w_te = sb("w_te", [P, TT, E])
        wT = sb("wT", [E, TOK])
        w_exp = sb("w_exp", [P, 2, TOK])
        y_sb = sb("y_sb", [P, TT, D])
        gi_dram = nc.dram_tensor("gi_scratch", [P, M, TOK], F32, kind="Internal").ap()
        w_dram = nc.dram_tensor("w_scratch", [E, TOK], F32, kind="Internal").ap()

        y_ps = ps("y_ps", [P, TT, 512])
        a_ps = ps("a_ps", [P, 512])
        b_ps = ps("b_ps", [P, 512])
        gh_ps = ps("gh_ps", [P, M, 2, B])
        misc_ps = ps("misc_ps", [P, 512])

        def gh_of(ffn):
            if ffn:
                return gh_ps[:, 0:K], gh_ps[:, K:2 * K], gh_ps[:, 2 * K:M]
            return gh_ps[:, 0:K], *(y_ps[:, t, 0:K * 2 * B].rearrange("p (k a b) -> p k a b", k=K, a=2)
                                    for t in range(2))

        GATE_BANKS = (misc_ps, b_ps, a_ps)
        GI_BANKS = (misc_ps, b_ps, misc_ps)

        whh_loaded = sem("whh_loaded")
        loaded = sem("loaded")
        const_ready = sem("const_ready")
        setup = sem("setup")
        mag_ready = sem("mag_ready")
        gh_ready = sem("gh_ready")
        gru_ops = sem("gru_ops")
        logged = sem("logged")
        sig_rz = sem("sig_rz")
        tanh_n = sem("tanh_n")
        x_loaded = sem("x_loaded")
        x_hi = sem("x_hi")
        x_lo = sem("x_lo")
        wi_loaded = [sem("wi_loaded_0"), sem("wi_loaded_1")]
        wi_hi = sem("wi_hi")
        gi_mm = sem("gi_mm")
        gi_out = [sem("gi_out_even"), sem("gi_out_odd")]
        gi_in = sem("gi_in")
        gi_ready = sem("gi_ready")
        wu_loaded = [sem("wu_loaded_0"), sem("wu_loaded_1")]
        wu_hi = sem("wu_hi")
        split = sem("split")
        wu_used = sem("wu_used")
        a_mm = sem("a_mm")
        b_mm = sem("b_mm")
        sig_a = sem("sig_a")
        ffn_ops = sem("ffn_ops")
        hid_hi = sem("hid_hi")
        f_hi = sem("f_hi")
        f_lo = sem("f_lo")
        score_mm = sem("score_mm")
        route_ops = sem("route_ops")
        score_T = sem("score_T")
        probs = sem("probs")
        w_T = sem("w_T")
        wT_out = sem("wT_out")
        w_loaded = [sem("w_even_loaded"), sem("w_odd_loaded")]
        y_read = sem("y_read")
        xres_loaded = sem("xres_loaded")
        stored = sem("stored")

        SC_W, SC_H, SC_INV, SC_IH, SC_NH, SC_PW, SC_PH = range(7)

        def scale(i):
            return sc[:, i:i + 1]

        def walk(eng, prologue, start, group, finish):
            prologue()
            start(1, False)
            for g in range(GROUPS):
                group(1, g, True, False, True)
            finish(1)
            with eng.Fori(2, CHUNKS - 1) as c:
                start(c, True)
                for g in range(GROUPS):
                    group(c, g, True, True, True)
                finish(c)
            start(CHUNKS - 1, False)
            for g in range(GROUPS):
                group(CHUNKS - 1, g, True, False, False)
            finish(CHUNKS - 1)
            start(CHUNKS, False)
            for g in range(GROUPS):
                group(CHUNKS, g, False, False, False)
            finish(CHUNKS)

        GATE_AT = {2 + 15 * c + MW * p + j: (c, p, j) for c in range(2) for p in range(WI) for j in range(MW)}
        WI_AT_STEP = {2: (0, 1), 4: (0, 2), 7: (0, 3), 10: (1, 0), 15: (1, 1), 19: (1, 2), 22: (1, 3)}
        X_AT_STEP, UNIT_AT_STEP, F_AT_STEP = 13, 26, 28

        def is_last(g):
            return g == GROUPS - 1

        def is_first(g, u):
            return g == 0 and u == 0

        def is_end(c, g):
            return isinstance(c, int) and c == CHUNKS and is_last(g)

        def route_banks(proj):
            return (b_ps, a_ps) if proj else (misc_ps, misc_ps)

        def step_no(c, g, s):
            return c * STEPS + g * GS + s

        def unit_no(c, g, u):
            return (c - 1) * UNITS + g * UG + u

        def wi_no(c, p):
            return (c + 1) * WI + p

        def gate_no(c, p, j):
            return (c + 1) * M + p * MW + j

        WI_AT = 4

        def raw_of(u):
            return (u - 1) % 2 if 0 < u <= WI_AT else 1 if u == 0 else u % 2

        def loaded_before(c, g, u):
            same = [v for v in range(1, UG + 1) if raw_of(v) == raw_of(u)]
            return ((c - 1) * GROUPS + g) * len(same) + same.index(u) + 1 + raw_of(u)

        def raw_of_wi(c, p):
            if in_prologue(c):
                return p % 2
            return 1 if isinstance(p, int) and p == 1 else 0

        def wi_parts(c, p):
            if isinstance(p, int) and (p == 1 or in_prologue(c) and p % 2):
                return wu_split[:, SPLITS - 1]
            return wi_split

        def spill_buf(m):
            return (sig, hid)[m % 2][:]

        def x_parts(n):
            return f_split if isinstance(n, int) and n == 0 else x_split

        def gru_count(t, name, beside):
            return GRU_OPS * t + (BESIDE if beside else ALONE).index(name) + 1 + CREDIT

        def pieces_before(c, g):
            first = 3 * WI + 1
            if isinstance(c, int) and c == 1:
                return first + g * UG
            steady = first + UNITS + 2
            if isinstance(c, int) and c >= CHUNKS - 1:
                return (steady + (CHUNKS - 3) * (WI + UNITS) - 1
                        + ((c - CHUNKS + 1) * GROUPS + g) * UG)
            return steady + (c - 2) * (WI + UNITS) + g * (1 + UG)

        def in_prologue(c):
            return isinstance(c, int) and c < 2

        CREDIT = 1

        def prev_in_ring(n, u):
            u %= UG
            return n - SPLITS if u >= SPLITS else n - u - (UG - u) % SPLITS - ((UG - u) % SPLITS == 0) * SPLITS

        N_ROUTE = 6 + 2 * TT + 3 * TT
        GAP = 5 + 2 * TT
        N_SMALL = 6 + K + E
        N_SETUP = N_SMALL + 14

        def settle(eng):
            if eng is nc.sync:
                eng.wait_ge(const_ready, 2)
            else:
                nc.vector.memset(spare[:], 0.0)

        block = ctx.enter_context(nc.Block())

        @block.sync
        def _(sp):
            sp.dma_start(h_now[:, 1], h0_feat).then_inc(loaded, 16)
            sp.dma_start(bias[:], b_feat).then_inc(loaded, 16)
            sp.dma_start(wg_raw[:], w_gate).then_inc(loaded, 16)

            def prologue():
                for c in (-1, 0, 1):
                    sp.wait_ge(x_lo, c + 1 + CREDIT)
                    sp.dma_start(x_raw[:], x_feat[c + 1]).then_inc(x_loaded, 16)
                    for p in range(WI):
                        n = wi_no(c, p)
                        load_wi(p, p % 2, max(0, n - 1))
                for m in range(M):
                    if m == M // 2:
                        sp.wait_ge(split, 3 * WI + CREDIT)
                        sp.dma_start(w_raw[:, 1], w_units[0]).then_inc(wu_loaded[1], 16)
                    sp.wait_ge(gi_ready, gate_no(1, 0, m) + 1 + CREDIT)
                    sp.dma_start(gi_dram[:, m], spill_buf(m)).then_inc(gi_out[m % 2], 16)

            def gi_back(part):
                if part == 0:
                    for half in range(2):
                        sp.wait_ge(gi_out[half], 16 * (M // 2))
                    sp.wait_ge(logged, STEPS)
                else:
                    sp.wait_ge(gi_in, 16 * part)
                rows = slice(part * MW, (part + 1) * MW)
                sp.dma_start(gi[:, 0, rows], gi_dram[:, rows]).then_inc(gi_in, 16)

            def load_x(n):
                settle(nc.sync)
                sp.wait_ge(x_lo, n + CREDIT)
                sp.dma_start(x_raw[:], x_feat[bass.ds(n % CHUNKS, 1)].rearrange("o p k t -> (o p) k t")
                             ).then_inc(x_loaded, 16)

            def load_wi(row, slot, pieces):
                settle(nc.sync)
                sp.wait_ge(split, pieces + CREDIT)
                sp.dma_start(w_raw[:, slot], w_inproj[bass.ds(row, 1)].rearrange("o p n -> (o p) n")
                             ).then_inc(wi_loaded[slot], 16)

            def start(c, proj):
                if proj:
                    load_wi(1, 1, pieces_before(c, 0) - 1)

            def group(c, g, rec, proj, nxt):
                if nxt and is_last(g):
                    load_x(c + 2)
                before = pieces_before(c, g)
                for u in range(1, UG + (not is_end(c, g))):
                    if proj and u == WI_AT + 1:
                        load_wi(2 + g, 0, before + WI_AT - 1)
                    if proj:
                        last = u - 2 + (u > WI_AT)
                    elif u <= WI_AT:
                        last = u - 2
                    else:
                        last = {WI_AT + 1: WI_AT, WI_AT + 2: WI_AT - 1}.get(u, u - 2)
                    settle(nc.sync)
                    sp.wait_ge(split, before + last + CREDIT)
                    row = g * UG + u if u < UG else g * -UG + UG
                    sp.dma_start(w_raw[:, raw_of(u)], w_units[bass.ds(row, 1)].rearrange("o p n -> (o p) n")
                                 ).then_inc(wu_loaded[raw_of(u)], 16)
                    if isinstance(c, int) and c == 1 and u in (3, 7):
                        gi_back(2 * g + u // 4)
                if nxt and is_last(g):
                    load_wi(0, 0, before + UG - (not proj))

            walk(sp, prologue, start, group, lambda c: None)

        @block.gpsimd
        def _(pool):
            nc.gpsimd.memset(ident[:], 0.0).then_inc(const_ready, 1)
            pool.wait_ge(const_ready, 1)
            nc.gpsimd.affine_select(out=ident[:], in_=ident[:], compare_op=ALU.not_equal, fill=1.0,
                                    base=0, pattern=[[-1, P]], channel_multiplier=1
                                    ).then_inc(const_ready, 1)
            pool.wait_ge(const_ready, 2)
            pool.wait_ge(setup, N_SMALL + 3)
            nc.gpsimd.partition_all_reduce(mags[:, 4:5], mags[:, 2:3], P, RMAX).then_inc(mag_ready, 1)
            nc.gpsimd.partition_all_reduce(mags[:, 5:6], mags[:, 3:4], P, RMAX).then_inc(mag_ready, 1)

            for f in range(CHUNKS):
                if f:
                    pool.wait_ge(stored, 16 * f)
                pool.dma_start(y_sb[:], x_tok[bass.ds(f * TOK, TOK), :].rearrange(
                    "(t p) d -> p t d", p=P)).then_inc(xres_loaded, 16)
                pool.wait_ge(route_ops, N_ROUTE * (f + 1))
                if f:
                    for e in range(2):
                        pool.wait_ge(w_loaded[e], 16 * (E // 2) * f)
                pool.dma_start(w_dram, wT[:]).then_inc(wT_out, 16)
                pool.wait_ge(wT_out, 16 * (f + 1))
                for e in range(E):
                    last = UNITS * f - 1 if e < 2 else UNITS * f + ((e - 1) * HE - 1) // P
                    pool.wait_ge(ffn_ops, FFN_OPS * (last + 1) + WEIGHTED)
                    pool.dma_start(w_exp[:, e % 2], w_dram[e:e + 1, :].to_broadcast([P, TOK])
                                   ).then_inc(w_loaded[e % 2], 16)
                pool.wait_ge(y_read, TT * (f + 1) + CREDIT)
                pool.dma_start(out[bass.ds(f * TOK, TOK), :].rearrange("(t p) d -> p t d", p=P),
                               y_sb[:]).then_inc(stored, 16)
            pool.wait_ge(stored, 16 * CHUNKS)

        @block.scalar
        def _(act):
            def prologue():
                split_x(0)
                act.dma_start(whh_raw[:], w_hh).then_inc(whh_loaded, 16)
                split_wi(-1, 0)
                split_wi(-1, 1)
                for p in range(WI):
                    for j in range(MW):
                        take_gi(-1, p, j, GATE_BANKS[j])
                    if p < 2:
                        split_wi(-1, 2 + p)
                    elif p == 2:
                        split_x(1)
                        split_wi(0, 0)
                for s in range(STEPS):
                    gru_acts(s, False)
                    if s in GATE_AT:
                        if s == min(GATE_AT):
                            act.wait_ge(setup, N_SETUP)
                        c, p, j = GATE_AT[s]
                        if c == 1 and p * MW + j >= 2:
                            m = p * MW + j
                            act.wait_ge(gi_out[m % 2], 16 * (m // 2))
                        take_gi(c, p, j, GATE_BANKS[j])
                    if s in WI_AT_STEP:
                        split_wi(*WI_AT_STEP[s])
                    if s == X_AT_STEP:
                        split_x(2)
                    if s == UNIT_AT_STEP:
                        split_wu(1, 0, 0)
                    if s == F_AT_STEP:
                        split_f(0, [0])
                for half in range(2):
                    act.wait_ge(gi_out[half], 16 * (M // 2))
                split_f(0, [1])

            def split_x(n):
                act.wait_ge(x_loaded, 16 * (n + 1))
                if not isinstance(n, int) or n > 1:
                    act.wait_ge(gi_mm, M * n + CREDIT)
                nc.scalar.copy(x_parts(n)[:, 0], x_raw[:]).then_inc(x_hi, 1)

            def split_wi(c, p):
                raw, dst = raw_of_wi(c, p), wi_parts(c, p)
                if in_prologue(c):
                    there = (c + 1) * (WI // 2) + p // 2 + 1
                elif raw:
                    there = 3 * (WI // 2) + c - 1
                else:
                    there = 3 * (WI // 2) + (c - 2) * (WI - 1) + (p - 1 if not isinstance(p, int) or p else 0) + 1
                act.wait_ge(wi_loaded[raw], 16 * there)
                used = gate_no(c, p, 0) - (MW if in_prologue(c) or isinstance(p, int) and p == 1 else 0)
                if raw and not in_prologue(c):
                    act.wait_ge(wu_used, SPLITS + UNITS * (c - 1))
                if not isinstance(used, int) or used > 0:
                    act.wait_ge(gi_mm, used + CREDIT)
                nc.scalar.copy(dst[:, 0], w_raw[:, raw]).then_inc(wi_hi, 1)

            def split_wu(c, g, u):
                n = unit_no(c, g, u)
                act.wait_ge(wu_loaded[raw_of(u)], 16 * (loaded_before(c, g, u) if u else 1))
                act.wait_ge(wu_used, prev_in_ring(n, u) + 1 + SPLITS)
                nc.scalar.copy(wu_split[:, u % UG % SPLITS, 0], w_raw[:, raw_of(u)]).then_inc(wu_hi, 1)

            def take_gi(c, p, j, src):
                act.wait_ge(gi_mm, gate_no(c, p, j) + 1 + CREDIT)
                m = p * MW + j
                dst = gi[:, bass.ds((c + 1) % 2, 1), bass.ds(m, 1), :]
                if isinstance(c, int) and c == 1:
                    dst = spill_buf(m)
                nc.scalar.activation(dst, src[:], ACT.Identity, bias=gi_bias[:, bass.ds(m, 1)]
                                     ).then_inc(gi_ready, 1)

            def start(c, proj):
                f = c - 1
                if proj:
                    for j in range(MW):
                        if j == MW - 1:
                            split_wi(c, 1)
                        take_gi(c, 0, j, GI_BANKS[j])
                act.wait_ge(route_ops, N_ROUTE * f + GAP)
                nc.scalar.activation(prob[:, 0], gap[:], ACT.Sigmoid).then_inc(probs, 1)
                nc.scalar.activation(prob[:, 1], gap[:], ACT.Sigmoid, scale=-1.0).then_inc(probs, 1)
                if proj:
                    for j in range(MW):
                        take_gi(c, 1, j, GI_BANKS[j])

            def split_f(f, halves=range(2)):
                for half in halves:
                    tokens = slice(half * GS * B, (half + 1) * GS * B)
                    act.wait_ge(logged, STEPS * f + GS * (half + 1))
                    if half == 0:
                        act.wait_ge(b_mm, UNITS * f + CREDIT)
                    nc.scalar.copy(f_split[:, 0, :, tokens], h_log[:, :, tokens]).then_inc(f_hi, 1)

            def gru_acts(t, beside):
                act.wait_ge(gru_ops, gru_count(t, "R_B", beside))
                nc.scalar.activation(rs[:], rpre[:, 1], ACT.Sigmoid).then_inc(sig_rz, 1)
                if not beside:
                    act.wait_ge(gru_ops, gru_count(t, "N_PRE", beside))
                    nc.scalar.activation(nt[:], npre[:], ACT.Tanh).then_inc(tanh_n, 1)
                act.wait_ge(gru_ops, gru_count(t, "Z_B", beside))
                nc.scalar.activation(zs[:], zpre[:, 1], ACT.Sigmoid).then_inc(sig_rz, 1)
                if beside:
                    act.wait_ge(gru_ops, gru_count(t, "N_PRE", beside))
                    nc.scalar.activation(nt[:], npre[:], ACT.Tanh).then_inc(tanh_n, 1)

            def after_down(c, g, u, proj, nxt):
                last = is_last(g)
                if u == UG - 4 and last and nxt and not proj:
                    split_x(c + 2)
                if u == UG - 2 and last and nxt:
                    split_wi(c + 1, 0)
                if u == UG - 1:
                    if last and not nxt and c < CHUNKS:
                        split_f(c)
                    if not is_end(c, g):
                        split_wu(c, g, UG)
                    if last and nxt:
                        split_f(c)

            def group(c, g, rec, proj, nxt):
                for s in range(GS):
                    if rec:
                        gru_acts(step_no(c, g, s), True)
                    for kind, i in blocks(proj, is_last(g))[s]:
                        n = unit_no(c, g, i)
                        if kind == "G":
                            take_gi(c, 2 + g, i, misc_ps)
                            if is_last(g) and i == MW - 1:
                                split_x(c + 2)
                        if kind == "Y":
                            after_down(c, g, i, proj, nxt)
                        if kind == "A":
                            if i + 1 < UG:
                                split_wu(c, g, i + 1)
                            act.wait_ge(a_mm, n + 1)
                            nc.scalar.activation(sig[:], a_ps[:], ACT.Sigmoid, scale=scale(SC_IH)
                                                 ).then_inc(sig_a, 1)
                        if kind == "B":
                            act.wait_ge(ffn_ops, FFN_OPS * (n + 1) + WEIGHTED)
                            act.wait_ge(wu_used, n + SPLITS - (1 if i else 0))
                            nc.scalar.copy(hid_split[:, i % 2, 0], hid[:]).then_inc(hid_hi, 1)
                            if i == WI_AT - 1 and proj:
                                split_wi(c, 2 + g)

            act.sem_inc(gi_ready, CREDIT)
            act.wait_ge(setup, N_SMALL)
            walk(act, prologue, start, group, lambda c: None)

        @block.vector
        def _(dve):
            done = [0]

            def chain(ins):
                done[0] += 1
                ins.then_inc(setup, 1)
                dve.wait_ge(setup, done[0])

            V = nc.vector
            dve.sem_inc(ffn_ops, FFN_OPS)
            for credited in (x_lo, split, gru_ops, y_read):
                dve.sem_inc(credited, CREDIT)
            dve.wait_ge(loaded, 48)
            chain(V.tensor_copy(gi_bias[:], bias[:, 0]))
            chain(V.tensor_tensor(gi_bias[:, 0:2 * K], bias[:, 0, 0:2 * K], bias[:, 1, 0:2 * K], ALU.add))
            chain(V.tensor_copy(bhn[:], bias[:, 1, 2 * K:M].unsqueeze(2).to_broadcast([P, K, B])))
            chain(V.memset(zeros_r[:].bitcast(F32), 0.0))
            for k in range(K):
                chain(V.tensor_copy(wg[:, k], zeros_r[:].bitcast(F32)))
            chain(V.tensor_copy(wg[:, :, 0:E], wg_raw[:]))
            chain(V.tensor_tensor(wg[:, :, E:2 * E], wg_raw[:], wg[:, :, 0:E].bitcast(F32), ALU.subtract))
            for e in range(E):
                chain(V.memset(iota_e[:, e:e + 1], float(e)))
            assert done[0] == N_SMALL, done[0]

            def scales():
                dve.wait_ge(whh_loaded, 16)
                chain(V.tensor_reduce(mags[:, 2:3], whh_raw[:], AX_XY, ALU.max, apply_absolute_value=True))
                chain(V.tensor_reduce(mags[:, 3:4], h_now[:, 1], AX_XY, ALU.max, apply_absolute_value=True))
                chain(V.tensor_scalar(mags[:, 3:4], mags[:, 3:4], 1.0, None, ALU.max))
                dve.wait_ge(mag_ready, 2)
                chain(V.tensor_scalar(mags[:, 4:6], mags[:, 4:6], 2.0 ** -40, None, ALU.max))
                chain(V.tensor_scalar(sc[:, SC_PW:SC_PH + 1].bitcast(I32), mags[:, 4:6].bitcast(I32),
                                      0x7F800000, None, ALU.bitwise_and))
                chain(V.tensor_scalar(sc[:, SC_W:SC_H + 1].bitcast(I32), sc[:, SC_PW:SC_PH + 1].bitcast(I32),
                                      -1.0, float((127 + 14 + 127) << 23), ALU.mult, ALU.add))
                chain(V.tensor_scalar(sc[:, SC_IH:SC_IH + 1], scale(SC_PH), 2.0 ** -14, None, ALU.mult))
                chain(V.tensor_scalar(sc[:, SC_INV:SC_INV + 1], scale(SC_PW), 2.0 ** -14, scale(SC_IH),
                                      ALU.mult, ALU.mult))
                chain(V.tensor_scalar(sc[:, SC_NH:SC_NH + 1], scale(SC_H), -1.0, None, ALU.mult))

            def recurrent_weights():
                chain(V.tensor_scalar(whh[:, 0], whh_raw[:], scale(SC_W), None, ALU.mult))
                chain(V.scalar_tensor_tensor(out=whh[:, 1], in0=whh_raw[:], scalar=scale(SC_W),
                                             in1=whh[:, 0], op0=ALU.mult, op1=ALU.subtract))
                chain(V.tensor_scalar(h_now[:, 0], h_now[:, 1], scale(SC_H), None, ALU.mult))
                chain(V.tensor_copy(h_parts[:, :, 0], h_now[:, 0]))
                chain(V.tensor_tensor(h_parts[:, :, 1], h_now[:, 0], h_parts[:, :, 0], ALU.subtract))
                assert done[0] == N_SETUP, done[0]

            def prologue():
                split_x(0)
                split_wi(-1, 0)
                split_wi(-1, 1)
                scales()
                split_wi(-1, 2)
                split_wi(-1, 3)
                recurrent_weights()
                for s in range(STEPS):
                    gru_step(0, 0, s, False)
                    if s == 0:
                        split_x(1)
                    if s == 1:
                        split_wi(0, 0)
                    if s - 1 in WI_AT_STEP:
                        split_wi(*WI_AT_STEP[s - 1])
                    if s - 1 == X_AT_STEP:
                        split_x(2)
                    if s - 1 == UNIT_AT_STEP:
                        split_wu(1, 0, 0)
                    if s - 1 == F_AT_STEP:
                        split_f(0, [0])
                split_f(0, [1])

            def split_x(n):
                x = x_parts(n)
                dve.wait_ge(x_hi, n + 1)
                V.tensor_tensor(x[:, 1], x_raw[:], x[:, 0].bitcast(F32), ALU.subtract).then_inc(x_lo, 1)

            def split_wi(c, p):
                dst = wi_parts(c, p)
                dve.wait_ge(wi_hi, wi_no(c, p) + 1)
                V.tensor_tensor(dst[:, 1], w_raw[:, raw_of_wi(c, p)], dst[:, 0].bitcast(F32), ALU.subtract
                                ).then_inc(split, 1)

            def split_wu(c, g, u):
                dve.wait_ge(wu_hi, unit_no(c, g, u) + 1)
                b = u % UG % SPLITS
                V.tensor_tensor(wu_split[:, b, 1], w_raw[:, raw_of(u)],
                                wu_split[:, b, 0].bitcast(F32), ALU.subtract
                                ).then_inc(split, 1)

            def route(c, proj):
                f = c - 1
                base = N_ROUTE * f
                n = [0]

                def op(ins, wait=True):
                    ins.then_inc(route_ops, 1)
                    n[0] += 1
                    if wait:
                        dve.wait_ge(route_ops, base + n[0])

                if proj:
                    split_wi(c, 1)
                dve.wait_ge(score_mm, f + 1)
                op(V.tensor_copy(scT[:], a_ps[0:2 * E, :]), False)
                dve.wait_ge(score_T, f + 1)
                halves = route_banks(proj)[0][:, 0:TT * 2 * E].rearrange("p (t e) -> p t e", t=TT)
                op(V.tensor_scalar(score1[:], halves[:, :, 0:E], scale(SC_IH), None, ALU.mult))
                op(V.scalar_tensor_tensor(out=score[:], in0=halves[:, :, E:2 * E], scalar=scale(SC_IH),
                                          in1=score1[:], op0=ALU.mult, op1=ALU.add))
                settle(nc.vector)
                for t in range(TT):
                    op(V.max(top[:, t], score[:, t]), t == TT - 1)
                settle(nc.vector)
                for t in range(TT):
                    op(V.max_index(top_i[:, t], top[:, t], score[:, t]), t == TT - 1)
                op(V.tensor_copy(top_f[:], top_i[:]))
                op(V.tensor_tensor(gap[:], top[:, :, 0], top[:, :, 1], ALU.subtract))
                assert n[0] == GAP
                dve.wait_ge(probs, 2 * (f + 1))
                for t in range(TT):
                    op(V.tensor_scalar(w_1[:, t], iota_e[:], top_f[:, t, 0:1], prob[:, 0, t:t + 1],
                                       ALU.is_equal, ALU.mult), False)
                for t in range(TT):
                    op(V.tensor_scalar(w_2[:, t], iota_e[:], top_f[:, t, 1:2], prob[:, 1, t:t + 1],
                                       ALU.is_equal, ALU.mult), t == TT - 1)
                for t in range(TT):
                    op(V.tensor_tensor(w_te[:, t], w_1[:, t], w_2[:, t], ALU.add), False)
                assert n[0] == N_ROUTE - 1, n[0]

            def take_wT(c, proj):
                dve.wait_ge(w_T, c)
                dve.wait_ge(xres_loaded, 16 * c)
                V.tensor_copy(wT[:], route_banks(proj)[1][0:E, :]).then_inc(route_ops, 1)

            def start(c, proj):
                if not isinstance(c, int):
                    dve.wait_ge(gi_in, 16 * WI)
                route(c, proj)
                if proj:
                    take_wT(c, proj)

            def split_f(f, halves=range(2)):
                for half in halves:
                    tokens = slice(half * GS * B, (half + 1) * GS * B)
                    dve.wait_ge(f_hi, 2 * f + half + 1)
                    V.tensor_tensor(f_split[:, 1, :, tokens], h_log[:, :, tokens],
                                    f_split[:, 0, :, tokens].bitcast(F32), ALU.subtract).then_inc(f_lo, 1)

            def gru_step(c, g, s, beside):
                t = step_no(c, g, s)
                now, new = s % 2, (s + 1) % 2
                at = g * (GS * B) + s * B
                gi_c = gi[:, bass.ds(c % 2, 1), :, bass.ds(at, B)].rearrange("p o m b -> p (o m) b")
                inv = scale(SC_INV)

                def after(k):
                    dve.wait_ge(gru_ops, gru_count(t, k, beside))

                def op(ins, n=1):
                    ins.then_inc(gru_ops, n)

                def first(dst, gh, base):
                    op(V.scalar_tensor_tensor(out=dst, in0=gh[:, :, 0, :], scalar=inv, in1=base,
                                              op0=ALU.mult, op1=ALU.add))

                def second(dst, gh, half):
                    op(V.scalar_tensor_tensor(out=dst, in0=gh[:, :, 1, :], scalar=inv, in1=half,
                                              op0=ALU.mult, op1=ALU.add))

                gh_r, gh_n, gh_z = gh_of(beside)
                gi_r, gi_z, gi_n = gi_c[:, 0:K], gi_c[:, K:2 * K], gi_c[:, 2 * K:M]
                if s == 0:
                    dve.wait_ge(gi_ready, M * (c + 1) + CREDIT)
                if beside:
                    dve.wait_ge(gh_ready, 3 * t + 3)
                    first(rpre[:, 0], gh_r, gi_r)
                    first(hn1[:], gh_n, bhn[:])
                    after("R_A")
                    second(rpre[:, 1], gh_r, rpre[:, 0])
                    after("HN_A")
                    second(hn[:], gh_n, hn1[:])
                    first(zpre[:, 0], gh_z, gi_z)
                    dve.wait_ge(sig_rz, 2 * t + 1)
                    after("HN_B")
                    op(V.tensor_tensor(rh[:], rs[:], hn[:], ALU.mult))
                    after("Z_A")
                    second(zpre[:, 1], gh_z, zpre[:, 0])
                    after("R_HN")
                    op(V.tensor_tensor(npre[:], rh[:], gi_n, ALU.add))
                    dve.wait_ge(sig_rz, 2 * t + 2)
                    op(V.tensor_tensor(zh[:], zs[:], h_now[:, now], ALU.mult))
                    op(V.tensor_scalar(omz[:], zs[:], scale(SC_NH), scale(SC_H), ALU.mult, ALU.add))
                    dve.wait_ge(tanh_n, t + 1)
                    after("ONE_Z")
                    op(V.tensor_tensor(nmix[:], nt[:], omz[:], ALU.mult))
                    after("N_MIX")
                    op(V.tensor_tensor(h_parts[:, :, 0], nmix[:], zh[:], ALU.add))
                    op(V.tensor_tensor(h_now[:, new], nmix[:], zh[:], ALU.add))
                else:
                    dve.wait_ge(gh_ready, 3 * t + 1)
                    first(rpre[:, 0], gh_r, gi_r)
                    after("R_A")
                    second(rpre[:, 1], gh_r, rpre[:, 0])
                    dve.wait_ge(gh_ready, 3 * t + 2)
                    first(hn1[:], gh_n, bhn[:])
                    after("HN_A")
                    second(hn[:], gh_n, hn1[:])
                    dve.wait_ge(sig_rz, 2 * t + 1)
                    after("HN_B")
                    op(V.tensor_tensor(rh[:], rs[:], hn[:], ALU.mult))
                    after("R_HN")
                    op(V.tensor_tensor(npre[:], rh[:], gi_n, ALU.add))
                    dve.wait_ge(gh_ready, 3 * t + 3)
                    first(zpre[:, 0], gh_z, gi_z)
                    after("Z_A")
                    second(zpre[:, 1], gh_z, zpre[:, 0])
                    dve.wait_ge(tanh_n, t + 1)
                    op(V.scalar_tensor_tensor(out=nmh[:], in0=nt[:], scalar=scale(SC_H), in1=h_now[:, now],
                                              op0=ALU.mult, op1=ALU.subtract))
                    dve.wait_ge(sig_rz, 2 * t + 2)
                    after("N_H")
                    op(V.tensor_tensor(znh[:], zs[:], nmh[:], ALU.mult))
                    after("Z_NH")
                    for dst in (h_parts[:, :, 0], h_now[:, new]):
                        op(V.scalar_tensor_tensor(out=dst, in0=nt[:], scalar=scale(SC_H), in1=znh[:],
                                                  op0=ALU.mult, op1=ALU.subtract))
                after("H_NEW")
                op(V.tensor_tensor(h_parts[:, :, 1], h_now[:, new], h_parts[:, :, 0], ALU.subtract),
                   1 if beside else 1 + len(BESIDE) - len(ALONE))
                V.tensor_copy(h_log[:, :, bass.ds(at, B)], h_now[:, new]).then_inc(logged, 1)

            def after_down(c, g, u, nxt):
                last = is_last(g)
                if u == UG - 3 and last and nxt:
                    split_x(c + 2)
                if u == UG - 2 and last and nxt:
                    split_wi(c + 1, 0)
                if u == UG - 1:
                    if last and not nxt and c < CHUNKS:
                        split_f(c)
                    if not is_end(c, g):
                        split_wu(c, g, UG)
                    if last and nxt:
                        split_f(c)

            def group(c, g, rec, proj, nxt):
                for s in range(GS):
                    if rec:
                        if is_first(g, s) and not proj:
                            take_wT(c, proj)
                        gru_step(c, g, s, True)
                    for kind, i in blocks(proj, is_last(g))[s]:
                        if kind == "Y":
                            after_down(c, g, i, nxt)
                        n = unit_no(c, g, i)
                        at = FFN_OPS * (n + 1)
                        if kind == "A":
                            early = ("Y", i - 2) not in blocks(proj, is_last(g))[s]
                            if i + 1 < UG and early:
                                split_wu(c, g, i + 1)
                            dve.wait_ge(sig_a, n + 1)
                            dve.wait_ge(ffn_ops, at)
                            V.scalar_tensor_tensor(out=hid[:], in0=a_ps[:], scalar=scale(SC_IH),
                                                   in1=sig[:], op0=ALU.mult, op1=ALU.mult
                                                   ).then_inc(ffn_ops, 1)
                            if is_first(g, i) and not proj and not rec:
                                take_wT(c, proj)
                            if i + 1 < UG and not early:
                                split_wu(c, g, i + 1)
                        if kind == "B":
                            dve.wait_ge(b_mm, n + 1 + CREDIT)
                            dve.wait_ge(ffn_ops, at + SILU)
                            V.scalar_tensor_tensor(out=hid[:], in0=b_ps[:], scalar=scale(SC_IH),
                                                   in1=hid[:], op0=ALU.mult, op1=ALU.mult
                                                   ).then_inc(ffn_ops, 1)
                            for e, r0, r1 in experts_of(i):
                                if e * HE >= i * P:
                                    dve.wait_ge(w_loaded[e % 2], 16 * ((c - 1) * (E // 2) + g * (EG // 2) + e // 2 + 1))
                                if r0 == 0:
                                    dve.wait_ge(ffn_ops, at + GATED)
                                ins = V.tensor_tensor(hid[r0:r1], hid[r0:r1], w_exp[r0:r1, e % 2], ALU.mult)
                            ins.then_inc(ffn_ops, 1)
                            dve.wait_ge(hid_hi, n + 1)
                            V.tensor_tensor(hid_split[:, i % 2, 1], hid[:],
                                            hid_split[:, i % 2, 0].bitcast(F32), ALU.subtract
                                            ).then_inc(ffn_ops, 1)
                            if i == WI_AT - 1 and proj:
                                split_wi(c, 2 + g)

            def finish(c):
                f = c - 1
                dve.wait_ge(wu_used, SPLITS + UNITS * (f + 1))
                dve.wait_ge(xres_loaded, 16 * (f + 1))
                for t in range(TT):
                    V.tensor_tensor(y_sb[:, t], y_ps[:, t], y_sb[:, t], ALU.add).then_inc(y_read, 1)

            walk(dve, prologue, start, group, finish)

        @block.tensor
        def _(pe):
            PARTS = ((0, 0), (0, 1), (1, 0))
            pe.sem_inc(wu_used, SPLITS)
            for credited in (gi_mm, b_mm):
                pe.sem_inc(credited, CREDIT)

            def recur(t, beside):
                pe.wait_ge(gru_ops, GRU_OPS * t + CREDIT)
                for dst, gate in zip(gh_of(beside), (0, 2, 1)):
                    for j in range(K):
                        m = gate * K + j
                        for k in range(K):
                            for part in range(2):
                                mm = pe.matmul(dst[:, j].rearrange("p a b -> p (a b)"),
                                               whh[:, part, k, m * P:(m + 1) * P],
                                               h_parts[:, k].rearrange("p a b -> p (a b)"),
                                               start=(k == 0 and part == 0), stop=(k == K - 1 and part == 1))
                    mm.then_inc(gh_ready, 1)

            def project(c, p, j, dst, before):
                if j == 0:
                    pe.wait_ge(x_lo, c + 2 + CREDIT)
                    if in_prologue(c):
                        at = wi_no(c, p) + 1
                    elif isinstance(p, int) and p < 2:
                        at = pieces_before(c, 0) + 2 * p - 2
                    else:
                        at = pieces_before(c, p - 2) + WI_AT + 1
                    pe.wait_ge(split, at + CREDIT)
                taken = gate_no(c, p, j) + 1 - before
                if not isinstance(taken, int) or taken > 0:
                    pe.wait_ge(gi_ready, taken + CREDIT)
                wi, x = wi_parts(c, p), x_parts(c + 1)
                for i, (a, b) in enumerate(PARTS):
                    for k in range(K):
                        mm = pe.matmul(dst[:], wi[:, a, (j * K + k) * P:(j * K + k + 1) * P],
                                       x[:, b, k], start=(i == 0 and k == 0),
                                       stop=(i == 2 and k == K - 1))
                mm.then_inc(gi_mm, 1)

            def up(c, g, u, dst, col, signal, proj):
                n = unit_no(c, g, u)
                if signal is a_mm:
                    if is_first(g, u) and proj:
                        pe.wait_ge(route_ops, N_ROUTE * c)
                    pe.wait_ge(split, pieces_before(c, g) + u + (proj and u > WI_AT) + CREDIT)
                    pe.wait_ge(ffn_ops, FFN_OPS * n + SILU)
                else:
                    if is_first(g, u) and proj:
                        pe.wait_ge(gi_ready, gate_no(c, 1, 2) + CREDIT)
                    pe.wait_ge(ffn_ops, FFN_OPS * n + GATED)
                for i, (a, b) in enumerate(PARTS):
                    for k in range(K):
                        mm = pe.matmul(dst[:], wu_split[:, u % SPLITS, a, col + k * P:col + (k + 1) * P],
                                       f_split[:, b, k], start=(i == 0 and k == 0),
                                       stop=(i == 2 and k == K - 1))
                mm.then_inc(signal, 1)

            def down(c, g, u):
                n = unit_no(c, g, u)
                pe.wait_ge(ffn_ops, FFN_OPS * (n + 1) + HID_LO)
                if is_first(g, u):
                    pe.wait_ge(y_read, TT * (c - 1) + CREDIT)
                for t in range(TT):
                    for a, b in PARTS:
                        mm = pe.matmul(y_ps[:, t], hid_split[:, u % 2, a, t * P:(t + 1) * P],
                                       wu_split[:, u % SPLITS, b, W3:W3 + D],
                                       start=(is_first(g, u) and (a, b) == PARTS[0]), stop=True,
                                       skip_group_check=True)
                mm.then_inc(wu_used, 1)

            def scores(f, proj):
                pe.wait_ge(f_lo, 2 * (f + 1))
                pe.wait_ge(ffn_ops, FFN_OPS * (UNITS * f + 1))
                for b in range(2):
                    for k in range(K):
                        mm = pe.matmul(a_ps[:], wg[:, k], f_split[:, b, k],
                                       start=(b == 0 and k == 0), stop=(b == 1 and k == K - 1))
                mm.then_inc(score_mm, 1)
                pe.wait_ge(route_ops, N_ROUTE * f + 1)
                for t in range(TT):
                    mm = pe.matmul(route_banks(proj)[0][:, t * 2 * E:(t + 1) * 2 * E], scT[:, t * P:(t + 1) * P],
                                   ident[0:2 * E, 0:2 * E])
                mm.then_inc(score_T, 1)

            def weights_T(f, proj):
                pe.wait_ge(route_ops, N_ROUTE * (f + 1) - 1)
                for t in range(TT):
                    mm = pe.matmul(route_banks(proj)[1][0:E, t * P:(t + 1) * P], w_te[:, t], ident[:])
                mm.then_inc(w_T, 1)

            def prologue():
                for p in range(WI):
                    for j in range(MW):
                        project(-1, p, j, GATE_BANKS[j], 3)
                pe.wait_ge(setup, N_SETUP)
                pe.wait_ge(const_ready, 2)
                for s in range(STEPS):
                    recur(s, False)
                    if s in GATE_AT:
                        c, p, j = GATE_AT[s]
                        project(c, p, j, GATE_BANKS[j], 3)

            def start(c, proj):
                if proj:
                    project(c, 0, 0, GI_BANKS[0], 1)
                    pe.wait_ge(ffn_ops, FFN_OPS * (UNITS * (c - 1) + 1))
                    project(c, 0, 1, GI_BANKS[1], 2)
                    project(c, 0, 2, GI_BANKS[2], 2)
                    pe.wait_ge(gi_ready, gate_no(c, 0, 2) + CREDIT)
                scores(c - 1, proj)
                if proj:
                    project(c, 1, 0, GI_BANKS[0], 1)
                    pe.wait_ge(route_ops, N_ROUTE * (c - 1) + 4)
                    project(c, 1, 1, GI_BANKS[1], 2)
                if proj:
                    weights_T(c - 1, proj)
                    project(c, 1, 2, GI_BANKS[2], 2)

            def group(c, g, rec, proj, nxt):
                for s in range(GS):
                    if rec:
                        recur(step_no(c, g, s), True)
                        if is_first(g, s) and not proj:
                            weights_T(c - 1, proj)
                    for kind, i in blocks(proj, is_last(g))[s]:
                        if kind == "G":
                            project(c, 2 + g, i, misc_ps, 1)
                        elif kind == "A":
                            up(c, g, i, a_ps, W1, a_mm, proj)
                        elif kind == "B":
                            up(c, g, i, b_ps, W2, b_mm, proj)
                            if is_first(g, i) and not proj and not rec:
                                weights_T(c - 1, proj)
                        elif kind == "Y":
                            down(c, g, i)

            walk(pe, prologue, start, group, lambda c: None)

def kernel(x, cond_2048, L0_cond_W_ih, L0_cond_W_hh, L0_cond_b_ih, L0_cond_b_hh,
           L0_ffn_Wg, L0_ffn_W1, L0_ffn_W2, L0_ffn_W3):
    import numpy as np
    import concourse.bacc as bacc
    from concourse import mybir as mb
    from concourse.bass_utils import run_bass_kernel_spmd

    x = np.asarray(x)
    B, T, D = x.shape
    K, M = D // P, 3 * D // P
    E, H, _ = np.asarray(L0_ffn_W1).shape
    STEPS, WI = 32, 4
    CHUNKS, TOK = T // STEPS, STEPS * B

    x_tok = np.ascontiguousarray(x.transpose(1, 0, 2)).reshape(T * B, D)
    x_feat = np.ascontiguousarray(x_tok.reshape(CHUNKS, TOK, K, P).transpose(0, 3, 2, 1))

    def feat(w):
        return np.ascontiguousarray(w.reshape(K, P, -1).transpose(1, 0, 2))

    w1, w2 = np.asarray(L0_ffn_W1).reshape(E * H, D), np.asarray(L0_ffn_W2).reshape(E * H, D)
    w3 = np.asarray(L0_ffn_W3).transpose(0, 2, 1).reshape(-1, P, D)

    def up_unit(w):
        return w.reshape(-1, P, K, P).transpose(0, 3, 2, 1).reshape(-1, P, K * P)

    w_units = np.ascontiguousarray(np.concatenate([up_unit(w1), up_unit(w2), w3], axis=2))
    w_ih = np.asarray(L0_cond_W_ih)
    w_inproj = np.ascontiguousarray(
        w_ih.reshape(K, P, WI, M // WI, P).transpose(2, 1, 3, 0, 4)).reshape(WI, P, -1)
    b_feat = np.ascontiguousarray(
        np.stack([np.asarray(L0_cond_b_ih), np.asarray(L0_cond_b_hh)]).reshape(2, M, P).transpose(2, 0, 1))

    arrays = {
        "x_feat": x_feat,
        "x_tok": x_tok,
        "h0_feat": feat(np.asarray(cond_2048).T),
        "w_hh": feat(np.asarray(L0_cond_W_hh)),
        "b_feat": b_feat,
        "w_gate": feat(np.asarray(L0_ffn_Wg).T),
        "w_units": w_units,
        "w_inproj": w_inproj,
    }
    nc = bacc.Bacc("TRN2", target_bir_lowering=False, num_devices=1, dynamic_dma_scratch_size=4096)
    args = [nc.dram_tensor(f"in_{n}", a.shape, mb.dt.from_np(a.dtype), kind="ExternalInput").ap()
            for n, a in arrays.items()]
    y = nc.dram_tensor("out_y", (T * B, D), mb.dt.float32, kind="ExternalOutput").ap()
    gru_moe_kernel(nc, *args, y)
    r = run_bass_kernel_spmd(nc, [{f"in_{n}": a for n, a in arrays.items()}], core_ids=[0])
    return np.ascontiguousarray(r.results[0]["out_y"].reshape(T, B, D).transpose(1, 0, 2))
```
